# Optimizing a Trainium2 kernel written in Bass

```python
import numpy as np
import jax
import jax.numpy as jnp

def _softmax(x, axis=-1):
    return jax.nn.softmax(x, axis=axis)

def _gelu(x):
    return jax.nn.gelu(x, approximate=True)

def _silu(x):
    return jax.nn.silu(x)

def _sigmoid(x):
    return jax.nn.sigmoid(x)

def _layernorm(x, axis=-1, eps=1e-05):
    m = jnp.mean(x, axis=axis, keepdims=True)
    v = jnp.var(x, axis=axis, keepdims=True)
    return (x - m) / jnp.sqrt(v + eps)

def _scatter_add(tgt, idx, src, axis=0):
    return tgt.at[idx].add(src)

def _segment_sum(src, seg, n):
    return jax.ops.segment_sum(src, seg, n)
kernel_name = 'mk_dlrm_tower_d1_rec_r8_5b3d21'

def setup_inputs(seed: int=0):
    np.random.seed(seed)
    _w = jnp.asarray

    def _rec_inputs():
        import jax
        import jax.numpy as jnp
        _tk = jax.random.key(seed)
        dense_ctx = jax.random.normal(jax.random.fold_in(_tk, 190), (512, 16), jnp.float32)
        ids = jnp.stack([jax.random.randint(jax.random.fold_in(_tk, 200 + f), (512,), 0, v, jnp.int32) for f, v in enumerate([125000, 12500, 125000, 12500, 125000, 12500, 12500, 1250, 1250, 1250, 1250, 1000, 12500, 1000, 125000, 1000, 12500, 12500, 125000, 12500, 1000, 1250, 1250, 1000, 1000, 125000, 1250, 1000, 1000, 1250, 12500, 1000, 1000, 1250, 12500, 1250, 1250, 12500, 1000, 12500])], axis=1)
        tbl_0 = 0.05 * jax.random.normal(jax.random.fold_in(_tk, 500 + 0), (125000, 32), jnp.float32)
        tbl_1 = 0.05 * jax.random.normal(jax.random.fold_in(_tk, 500 + 1), (12500, 32), jnp.float32)
        tbl_2 = 0.05 * jax.random.normal(jax.random.fold_in(_tk, 500 + 2), (125000, 32), jnp.float32)
        tbl_3 = 0.05 * jax.random.normal(jax.random.fold_in(_tk, 500 + 3), (12500, 32), jnp.float32)
        tbl_4 = 0.05 * jax.random.normal(jax.random.fold_in(_tk, 500 + 4), (125000, 32), jnp.float32)
        tbl_5 = 0.05 * jax.random.normal(jax.random.fold_in(_tk, 500 + 5), (12500, 32), jnp.float32)
        tbl_6 = 0.05 * jax.random.normal(jax.random.fold_in(_tk, 500 + 6), (12500, 32), jnp.float32)
        tbl_7 = 0.05 * jax.random.normal(jax.random.fold_in(_tk, 500 + 7), (1250, 32), jnp.float32)
        tbl_8 = 0.05 * jax.random.normal(jax.random.fold_in(_tk, 500 + 8), (1250, 32), jnp.float32)
        tbl_9 = 0.05 * jax.random.normal(jax.random.fold_in(_tk, 500 + 9), (1250, 32), jnp.float32)
        tbl_10 = 0.05 * jax.random.normal(jax.random.fold_in(_tk, 500 + 10), (1250, 32), jnp.float32)
        tbl_11 = 0.05 * jax.random.normal(jax.random.fold_in(_tk, 500 + 11), (1000, 32), jnp.float32)
        tbl_12 = 0.05 * jax.random.normal(jax.random.fold_in(_tk, 500 + 12), (12500, 32), jnp.float32)
        tbl_13 = 0.05 * jax.random.normal(jax.random.fold_in(_tk, 500 + 13), (1000, 32), jnp.float32)
        tbl_14 = 0.05 * jax.random.normal(jax.random.fold_in(_tk, 500 + 14), (125000, 32), jnp.float32)
        tbl_15 = 0.05 * jax.random.normal(jax.random.fold_in(_tk, 500 + 15), (1000, 32), jnp.float32)
        tbl_16 = 0.05 * jax.random.normal(jax.random.fold_in(_tk, 500 + 16), (12500, 32), jnp.float32)
        tbl_17 = 0.05 * jax.random.normal(jax.random.fold_in(_tk, 500 + 17), (12500, 32), jnp.float32)
        tbl_18 = 0.05 * jax.random.normal(jax.random.fold_in(_tk, 500 + 18), (125000, 32), jnp.float32)
        tbl_19 = 0.05 * jax.random.normal(jax.random.fold_in(_tk, 500 + 19), (12500, 32), jnp.float32)
        tbl_20 = 0.05 * jax.random.normal(jax.random.fold_in(_tk, 500 + 20), (1000, 32), jnp.float32)
        tbl_21 = 0.05 * jax.random.normal(jax.random.fold_in(_tk, 500 + 21), (1250, 32), jnp.float32)
        tbl_22 = 0.05 * jax.random.normal(jax.random.fold_in(_tk, 500 + 22), (1250, 32), jnp.float32)
        tbl_23 = 0.05 * jax.random.normal(jax.random.fold_in(_tk, 500 + 23), (1000, 32), jnp.float32)
        tbl_24 = 0.05 * jax.random.normal(jax.random.fold_in(_tk, 500 + 24), (1000, 32), jnp.float32)
        tbl_25 = 0.05 * jax.random.normal(jax.random.fold_in(_tk, 500 + 25), (125000, 32), jnp.float32)
        tbl_26 = 0.05 * jax.random.normal(jax.random.fold_in(_tk, 500 + 26), (1250, 32), jnp.float32)
        tbl_27 = 0.05 * jax.random.normal(jax.random.fold_in(_tk, 500 + 27), (1000, 32), jnp.float32)
        tbl_28 = 0.05 * jax.random.normal(jax.random.fold_in(_tk, 500 + 28), (1000, 32), jnp.float32)
        tbl_29 = 0.05 * jax.random.normal(jax.random.fold_in(_tk, 500 + 29), (1250, 32), jnp.float32)
        tbl_30 = 0.05 * jax.random.normal(jax.random.fold_in(_tk, 500 + 30), (12500, 32), jnp.float32)
        tbl_31 = 0.05 * jax.random.normal(jax.random.fold_in(_tk, 500 + 31), (1000, 32), jnp.float32)
        tbl_32 = 0.05 * jax.random.normal(jax.random.fold_in(_tk, 500 + 32), (1000, 32), jnp.float32)
        tbl_33 = 0.05 * jax.random.normal(jax.random.fold_in(_tk, 500 + 33), (1250, 32), jnp.float32)
        tbl_34 = 0.05 * jax.random.normal(jax.random.fold_in(_tk, 500 + 34), (12500, 32), jnp.float32)
        tbl_35 = 0.05 * jax.random.normal(jax.random.fold_in(_tk, 500 + 35), (1250, 32), jnp.float32)
        tbl_36 = 0.05 * jax.random.normal(jax.random.fold_in(_tk, 500 + 36), (1250, 32), jnp.float32)
        tbl_37 = 0.05 * jax.random.normal(jax.random.fold_in(_tk, 500 + 37), (12500, 32), jnp.float32)
        tbl_38 = 0.05 * jax.random.normal(jax.random.fold_in(_tk, 500 + 38), (1000, 32), jnp.float32)
        tbl_39 = 0.05 * jax.random.normal(jax.random.fold_in(_tk, 500 + 39), (12500, 32), jnp.float32)
        _rk = jax.random.fold_in(_tk, 7)
        W_top1 = 0.049029 * jax.random.normal(jax.random.fold_in(_tk, 801), (416, 512), jnp.float32)
        W_top2 = 0.0441942 * jax.random.normal(jax.random.fold_in(_tk, 802), (512, 256), jnp.float32)
        W_top3 = 0.0625 * jax.random.normal(jax.random.fold_in(_tk, 803), (256, 1), jnp.float32)
        b_top1 = jnp.zeros((512,), jnp.float32)
        b_top2 = jnp.zeros((256,), jnp.float32)
        return (dense_ctx, ids, tbl_0, tbl_1, tbl_2, tbl_3, tbl_4, tbl_5, tbl_6, tbl_7, tbl_8, tbl_9, tbl_10, tbl_11, tbl_12, tbl_13, tbl_14, tbl_15, tbl_16, tbl_17, tbl_18, tbl_19, tbl_20, tbl_21, tbl_22, tbl_23, tbl_24, tbl_25, tbl_26, tbl_27, tbl_28, tbl_29, tbl_30, tbl_31, tbl_32, tbl_33, tbl_34, tbl_35, tbl_36, tbl_37, tbl_38, tbl_39, W_top1, b_top1, W_top2, b_top2, W_top3)
    dense_ctx, ids, tbl_0, tbl_1, tbl_2, tbl_3, tbl_4, tbl_5, tbl_6, tbl_7, tbl_8, tbl_9, tbl_10, tbl_11, tbl_12, tbl_13, tbl_14, tbl_15, tbl_16, tbl_17, tbl_18, tbl_19, tbl_20, tbl_21, tbl_22, tbl_23, tbl_24, tbl_25, tbl_26, tbl_27, tbl_28, tbl_29, tbl_30, tbl_31, tbl_32, tbl_33, tbl_34, tbl_35, tbl_36, tbl_37, tbl_38, tbl_39, W_top1, b_top1, W_top2, b_top2, W_top3 = _rec_inputs()

    def _L0_rec_setup():
        import jax, jax.numpy as jnp
        import numpy as np
        B, F0, K = (256, 40, 32)
        CIN_SIZE = [200, 200]

        def _cin(inputs, params):
            Bb, F0_, Kk = inputs.shape
            res = inputs
            outs = []
            for wq, wk, wv, cw in params:
                x0_wk = inputs * wk
                x0_wv = inputs * wv
                xi_wq = res * wq
                phi = jnp.einsum('bfk,bgk->bkfg', x0_wk, xi_wq)
                alpha = jax.nn.softmax(phi, axis=2)
                x = alpha * jnp.transpose(x0_wv, (0, 2, 1))[:, :, :, None]
                x = x.reshape(Bb, Kk, -1)
                out = jnp.einsum('bkc,cj->bjk', x, cw[0])
                outs.append(out)
                res = out
            cat = jnp.concatenate(outs, axis=1)
            return cat.sum(axis=-1)
        key = jax.random.key(seed)
        ks = jax.random.split(key, 1 + 4 * len(CIN_SIZE))
        field_num = [F0] + CIN_SIZE
        d = {'inputs': jax.random.normal(ks[0], (B, F0, K), dtype=jnp.float32)}
        for i in range(len(CIN_SIZE)):
            d[f'wq{i}'] = jax.random.normal(ks[1 + 4 * i], (1, field_num[i], K), dtype=jnp.float32) * 0.05
            d[f'wk{i}'] = jax.random.normal(ks[2 + 4 * i], (1, F0, K), dtype=jnp.float32) * 0.05
            d[f'wv{i}'] = jax.random.normal(ks[3 + 4 * i], (1, F0, K), dtype=jnp.float32) * 0.05
            lim = (6.0 / (F0 * field_num[i] + field_num[i + 1])) ** 0.5
            d[f'cw{i}'] = jax.random.uniform(ks[4 + 4 * i], (1, F0 * field_num[i], field_num[i + 1]), minval=-lim, maxval=lim, dtype=jnp.float32)
        return d
    _L0_rec_all = _L0_rec_setup()
    _L0_rec_in = {k: v for k, v in _L0_rec_all.items() if k in ('wq0', 'wk0', 'wv0', 'cw0', 'wq1', 'wk1', 'wv1', 'cw1')}
    del _L0_rec_all
    return {'dense_ctx': dense_ctx, 'ids': ids, 'tbl_0': tbl_0, 'tbl_1': tbl_1, 'tbl_2': tbl_2, 'tbl_3': tbl_3, 'tbl_4': tbl_4, 'tbl_5': tbl_5, 'tbl_6': tbl_6, 'tbl_7': tbl_7, 'tbl_8': tbl_8, 'tbl_9': tbl_9, 'tbl_10': tbl_10, 'tbl_11': tbl_11, 'tbl_12': tbl_12, 'tbl_13': tbl_13, 'tbl_14': tbl_14, 'tbl_15': tbl_15, 'tbl_16': tbl_16, 'tbl_17': tbl_17, 'tbl_18': tbl_18, 'tbl_19': tbl_19, 'tbl_20': tbl_20, 'tbl_21': tbl_21, 'tbl_22': tbl_22, 'tbl_23': tbl_23, 'tbl_24': tbl_24, 'tbl_25': tbl_25, 'tbl_26': tbl_26, 'tbl_27': tbl_27, 'tbl_28': tbl_28, 'tbl_29': tbl_29, 'tbl_30': tbl_30, 'tbl_31': tbl_31, 'tbl_32': tbl_32, 'tbl_33': tbl_33, 'tbl_34': tbl_34, 'tbl_35': tbl_35, 'tbl_36': tbl_36, 'tbl_37': tbl_37, 'tbl_38': tbl_38, 'tbl_39': tbl_39, 'W_top1': W_top1, 'b_top1': b_top1, 'W_top2': W_top2, 'b_top2': b_top2, 'W_top3': W_top3, 'L0_rec_wq0': _L0_rec_in['wq0'], 'L0_rec_wk0': _L0_rec_in['wk0'], 'L0_rec_wv0': _L0_rec_in['wv0'], 'L0_rec_cw0': _L0_rec_in['cw0'], 'L0_rec_wq1': _L0_rec_in['wq1'], 'L0_rec_wk1': _L0_rec_in['wk1'], 'L0_rec_wv1': _L0_rec_in['wv1'], 'L0_rec_cw1': _L0_rec_in['cw1']}

def reference(dense_ctx, ids, tbl_0, tbl_1, tbl_2, tbl_3, tbl_4, tbl_5, tbl_6, tbl_7, tbl_8, tbl_9, tbl_10, tbl_11, tbl_12, tbl_13, tbl_14, tbl_15, tbl_16, tbl_17, tbl_18, tbl_19, tbl_20, tbl_21, tbl_22, tbl_23, tbl_24, tbl_25, tbl_26, tbl_27, tbl_28, tbl_29, tbl_30, tbl_31, tbl_32, tbl_33, tbl_34, tbl_35, tbl_36, tbl_37, tbl_38, tbl_39, W_top1, b_top1, W_top2, b_top2, W_top3, L0_rec_wq0, L0_rec_wk0, L0_rec_wv0, L0_rec_cw0, L0_rec_wq1, L0_rec_wk1, L0_rec_wv1, L0_rec_cw1):
    import jax
    import jax.numpy as jnp

    def _L0_rec_ref(inputs, wq0, wk0, wv0, cw0, wq1, wk1, wv1, cw1):
        import jax, jax.numpy as jnp
        import numpy as np
        B, F0, K = (256, 40, 32)
        CIN_SIZE = [200, 200]

        def _cin(inputs, params):
            Bb, F0_, Kk = inputs.shape
            res = inputs
            outs = []
            for wq, wk, wv, cw in params:
                x0_wk = inputs * wk
                x0_wv = inputs * wv
                xi_wq = res * wq
                phi = jnp.einsum('bfk,bgk->bkfg', x0_wk, xi_wq)
                alpha = jax.nn.softmax(phi, axis=2)
                x = alpha * jnp.transpose(x0_wv, (0, 2, 1))[:, :, :, None]
                x = x.reshape(Bb, Kk, -1)
                out = jnp.einsum('bkc,cj->bjk', x, cw[0])
                outs.append(out)
                res = out
            cat = jnp.concatenate(outs, axis=1)
            return cat.sum(axis=-1)
        return _cin(inputs, [(wq0, wk0, wv0, cw0), (wq1, wk1, wv1, cw1)])
    e = jnp.stack([tbl_0[ids[:, 0]], tbl_1[ids[:, 1]], tbl_2[ids[:, 2]], tbl_3[ids[:, 3]], tbl_4[ids[:, 4]], tbl_5[ids[:, 5]], tbl_6[ids[:, 6]], tbl_7[ids[:, 7]], tbl_8[ids[:, 8]], tbl_9[ids[:, 9]], tbl_10[ids[:, 10]], tbl_11[ids[:, 11]], tbl_12[ids[:, 12]], tbl_13[ids[:, 13]], tbl_14[ids[:, 14]], tbl_15[ids[:, 15]], tbl_16[ids[:, 16]], tbl_17[ids[:, 17]], tbl_18[ids[:, 18]], tbl_19[ids[:, 19]], tbl_20[ids[:, 20]], tbl_21[ids[:, 21]], tbl_22[ids[:, 22]], tbl_23[ids[:, 23]], tbl_24[ids[:, 24]], tbl_25[ids[:, 25]], tbl_26[ids[:, 26]], tbl_27[ids[:, 27]], tbl_28[ids[:, 28]], tbl_29[ids[:, 29]], tbl_30[ids[:, 30]], tbl_31[ids[:, 31]], tbl_32[ids[:, 32]], tbl_33[ids[:, 33]], tbl_34[ids[:, 34]], tbl_35[ids[:, 35]], tbl_36[ids[:, 36]], tbl_37[ids[:, 37]], tbl_38[ids[:, 38]], tbl_39[ids[:, 39]]], axis=1)
    z = _L0_rec_ref(e, L0_rec_wq0, L0_rec_wk0, L0_rec_wv0, L0_rec_cw0, L0_rec_wq1, L0_rec_wk1, L0_rec_wv1, L0_rec_cw1)
    z = z.reshape(z.shape[0], -1)
    h = jnp.concatenate([z, dense_ctx], axis=1)
    h = jnp.maximum(h @ W_top1 + b_top1, 0.0)
    h = jnp.maximum(h @ W_top2 + b_top2, 0.0)
    y = h @ W_top3
    return y

_drawn_inputs = setup_inputs


def setup_inputs(seed=0):
    import zlib

    import numpy as np

    out = dict(_drawn_inputs(seed))
    spreads = {'b_top1': (0.0, 0.1), 'b_top2': (0.0, 0.1)}
    factors = {'tbl_0': 8.0,
     'tbl_1': 8.0,
     'tbl_2': 8.0,
     'tbl_3': 8.0,
     'tbl_4': 8.0,
     'tbl_5': 8.0,
     'tbl_6': 8.0,
     'tbl_7': 8.0,
     'tbl_8': 8.0,
     'tbl_9': 8.0,
     'tbl_10': 8.0,
     'tbl_11': 8.0,
     'tbl_12': 8.0,
     'tbl_13': 8.0,
     'tbl_14': 8.0,
     'tbl_15': 8.0,
     'tbl_16': 8.0,
     'tbl_17': 8.0,
     'tbl_18': 8.0,
     'tbl_19': 8.0,
     'tbl_20': 8.0,
     'tbl_21': 8.0,
     'tbl_22': 8.0,
     'tbl_23': 8.0,
     'tbl_24': 8.0,
     'tbl_25': 8.0,
     'tbl_26': 8.0,
     'tbl_27': 8.0,
     'tbl_28': 8.0,
     'tbl_29': 8.0,
     'tbl_30': 8.0,
     'tbl_31': 8.0,
     'tbl_32': 8.0,
     'tbl_33': 8.0,
     'tbl_34': 8.0,
     'tbl_35': 8.0,
     'tbl_36': 8.0,
     'tbl_37': 8.0,
     'tbl_38': 8.0,
     'tbl_39': 8.0,
     'L0_rec_wq0': 8.0,
     'L0_rec_wk0': 8.0,
     'L0_rec_wv0': 8.0,
     'L0_rec_cw0': 8.0,
     'L0_rec_wq1': 64.0,
     'L0_rec_wk1': 64.0,
     'L0_rec_wv1': 8.0,
     'L0_rec_cw1': 8.0}
    for name, (base, spread) in spreads.items():
        noise = np.random.default_rng([zlib.crc32(name.encode()), seed]).standard_normal(out[name].shape)
        drawn = base * np.exp(spread * noise) if base else spread * noise
        out[name] = jnp.asarray(drawn.astype(out[name].dtype))
    for name, factor in factors.items():
        out[name] = (out[name] * factor).astype(out[name].dtype)
    return out
```

```python
from contextlib import ExitStack

import concourse.bass as bass
from concourse import mybir

ALU = mybir.AluOpType
ACT = mybir.ActivationFunctionType
F32 = mybir.dt.float32
I32 = mybir.dt.int32
AX_X = mybir.AxisListType.X

P = 128
B, F, K, G = 512, 40, 32, 200
NB = P // K
FJ, FQ = P // K, F * K // P
C0 = F * F
NCH = -(-C0 // P)
TAIL = C0 - (NCH - 1) * P
GROUPS = [range(0, 4), range(4, 8), range(8, 11), range(11, NCH)]
PAIRS = B // (2 * NB)
H = G // 2
NDENSE, N1, N2 = 16, 512, 256
BPAD = B + 4 * NB
CHUNKS = B // P
FB = 5
BLOCKS = F // FB


def cin_tower(nc, ids, tables, dense, wa, wq1, wd, cw0, cw1, w1, b1, w2, b2, w3, consts, x_scratch, out):
    with ExitStack() as ctx:
        def sb(name, shape, dt=F32):
            return ctx.enter_context(nc.sbuf_tensor(name, shape, dt))

        def bank(name):
            return ctx.enter_context(nc.psum_tensor(name, [P, 512], F32))

        def sem(name):
            return ctx.enter_context(nc.semaphore(name))

        cst = sb("cst", [P, P + K + NB + NB * P])
        ident = cst[:, 0:P]
        delta = cst[:, P:P + K]
        quad = cst[:, P + K:P + K + NB]
        spread = cst[:, P + K + NB:].rearrange("p (i m) -> p i m", i=NB)
        idx = sb("idx", [P, CHUNKS, F], I32)
        gath = sb("gath", [P, 2, F * K])
        e_field = sb("e_field", [P, BPAD, FQ])
        e_row = sb("e_row", [P, 2, F])
        w_row = sb("w_row", [P, 4, F])
        w_field = sb("w_field", [P, 2, FQ])
        wq1_row = sb("wq1_row", [P, G])
        a0a1c0v0 = sb("a0a1c0v0", [P, 4, 2, F])
        ends = sb("ends", [P, 2, 2, 2])
        hold = sb("hold", [P, 2])
        mlo = sb("mlo", [P, 2, F])
        mhi = sb("mhi", [P, 2, F])
        m0 = sb("m0", [P, 2, F])
        x0 = sb("x0", [P, 2, C0])
        sum0 = sb("sum0", [P, F])
        rec0 = sb("rec0", [P, F])
        x0T = sb("x0T", [P, NCH, P])
        cw0_sb = sb("cw0_sb", [P, NCH, G])
        out0 = sb("out0", [P, G])
        low1 = sb("low1", [P, G])
        cm = sb("cm", [P, 2, 2, G])
        m_field = sb("m_field", [P, 2, G])
        a1 = sb("a1", [P, 8, FQ])
        v1 = sb("v1", [P, 8, FQ])
        ex = sb("ex", [P, 8, FQ * G])
        rec1 = sb("rec1", [P, G])
        rec_field = sb("rec_field", [P, 8, G])
        vsel = sb("vsel", [P, 8 * (FQ * 32 + 4)])
        xsum = sb("xsum", [P, 500])
        z0T = sb("z0T", [H, 2, B + 2 * NB])
        ex_flat = ex[:].rearrange("p b x -> p (b x)")
        xblk = ex_flat[:, 0:2 * CHUNKS * FB * G].rearrange("p (a c x) -> p a c x", a=2, c=CHUNKS)
        cwblk = ex_flat[0:H, 8 * FQ * G - 4 * FB * G:8 * FQ * G].rearrange("p (a u j) -> p a u j", a=2, j=G)
        xT = x0T[0:H, 0:8, :].rearrange("p (a c) b -> p a (c b)", a=2)
        zeros = sb("zeros", [H, H])
        z1T = sb("z1T", [H, 2, B])
        w1_sb = sb("w1_sb", [H, 5, N1])
        w2_sb = sb("w2_sb", [P, N1 // P, N2])
        w3_sb = sb("w3_sb", [P, N2 // P])
        b1_sb = sb("b1_sb", [P, N1 // P])
        b2_sb = sb("b2_sb", [P, N2 // P])
        dense_sb = sb("dense_sb", [P, CHUNKS, NDENSE])
        denseT = sb("denseT", [NDENSE, B])
        h1T = gath[:].rearrange("p a b -> p (a b)")[:, 0:4 * 512].rearrange("p (c b) -> p c b", b=B)
        h2T = x0[:].rearrange("p a b -> p (a b)")[:, 0:2 * 512].rearrange("p (c b) -> p c b", b=B)
        y_sb = sb("y_sb", [1, B])

        pT = [bank("pT0"), bank("pT1")]
        pO = bank("pO")
        pC = [bank("pC0"), bank("pC1")]
        pS = bank("pS")
        pR = bank("pR")
        pX = bank("pX")

        names = """loaded_idx loaded loaded_top gathered_even gathered_odd e_turned e_kept padded zeroed
            erow_made abc_made phi0_made phi0_shifted exp0_made x0_scaled x0_made
            x0_turned x0T_kept out0_made out0_kept z0_made z0_kept cm_made
            cm_spread m_kept phi1_made exp1_made sums_made rec_made rec_spread rec_kept
            x1_by_pool x1_by_dve vsel_lo vsel_hi x_summed xsum_kept spilled
            dve_step xblk_even xblk_odd cwblk_even cwblk_odd xb_turned xT_act xT_dve block_used z1_made z1_kept
            dense_turned dense_kept h1_made h1_kept h2_made h2_kept y_made y_kept y_stored"""
        s = {n: sem(n) for n in names.split()}

        gathered = [s["gathered_even"], s["gathered_odd"]]
        xblk_loaded = [s["xblk_even"], s["xblk_odd"]]
        cwblk_loaded = [s["cwblk_even"], s["cwblk_odd"]]

        vflat = vsel[:]
        vdiag = vflat.rearrange("p (b x) -> p b x", x=FQ * 32 + 4)[:, :, 0:FQ * 32].rearrange(
            "p b (f c) -> p b f c", c=32)[:, :, :, 0:4]
        ex4 = ex[:].rearrange("p b (f g) -> p b f g", g=G)
        n_loads = 6

        block = ctx.enter_context(nc.Block())

        STEPS_HEAD, STEPS_TURN = 5 + 2 * 2 + 2 + 1, 1 + 5 + 2 * 2 + 2 * 2 + 1 + 1

        @block.sync
        def _(sp):
            sp.dma_start(idx[:], ids.rearrange("(c p) f -> p c f", p=P)).then_inc(s["loaded_idx"], 16)
            for dst, src in ((cst[:], consts), (w_row[:], wa), (w_field[:], wd), (wq1_row[:], wq1),
                             (cw0_sb[:, 0:NCH - 1, :], cw0[0:(NCH - 1) * P, :].rearrange("(c p) j -> p c j", p=P)),
                             (cw0_sb[0:TAIL, NCH - 1, :], cw0[(NCH - 1) * P:, :])):
                sp.dma_start(dst, src).then_inc(s["loaded"], 16)
            for dst, src in ((w1_sb[:, 0:4, :], w1[0:4 * H, :].rearrange("(c p) j -> p c j", p=H)),
                             (w1_sb[0:NDENSE, 4, :], w1[4 * H:, :]),
                             (w2_sb[:], w2.rearrange("(c p) j -> p c j", p=P)),
                             (w3_sb[:], w3),
                             (b1_sb[:], b1),
                             (b2_sb[:], b2),
                             (dense_sb[:], dense.rearrange("(c p) j -> p c j", p=P))):
                sp.dma_start(dst, src).then_inc(s["loaded_top"], 16)

            def spill(m):
                sp.wait_ge(s["xsum_kept"], m + 1)
                sp.dma_start(x_scratch[:, bass.ds(m * 8, 8), :, :].rearrange("c b j x -> c (b j) x"),
                             xsum[:]).then_inc(s["spilled"], 16)

            with sp.Fori(0, PAIRS) as m:
                spill(m)
            sp.wait_ge(s["spilled"], 16 * PAIRS)

            def load_block(c, buf):
                sp.dma_start(xblk[:, buf, :, :],
                             x_scratch[bass.ds(c, 1), :, 2 * buf:2 * buf + 2, :].rearrange(
                                 "c (n p) j x -> p (c n) (j x)", p=P)).then_inc(xblk_loaded[buf], 16)
                sp.dma_start(cwblk[:, buf, :, :],
                             cw1[bass.ds(c * 2 + buf, 1), :, :, :].rearrange("c u p j -> p (c u) j")
                             ).then_inc(cwblk_loaded[buf], 16)

            load_block(0, 0)
            load_block(0, 1)
            with sp.Fori(1, BLOCKS // 2) as t:
                for buf in range(2):
                    sp.wait_ge(s["block_used"], t * 2 + buf - 1)
                    load_block(t, buf)
            sp.wait_ge(s["y_kept"], 1)
            sp.dma_start(out.rearrange("b o -> o b"), y_sb[:]).then_inc(s["y_stored"], 16)
            sp.wait_ge(s["y_stored"], 16)

        @block.gpsimd
        def _(pool):
            pool.wait_ge(s["loaded_idx"], 16)
            for c in range(CHUNKS):
                if c >= 2:
                    pool.wait_ge(s["e_turned"], 3 * (c - 1))
                for f in range(F):
                    pool.indirect_dma_start(
                        out=gath[:, c % 2, f * K:(f + 1) * K], out_offset=None, in_=tables[f],
                        in_offset=bass.IndirectOffsetOnAxis(ap=idx[:, c, f:f + 1], axis=0),
                    ).then_inc(gathered[c % 2], 16)

            def weighted(p):
                pool.wait_ge(s["erow_made"], p + 1)
                if not isinstance(p, int) or p > 0:
                    pool.wait_ge(s["x0_made"], p * 2)
                pool.tensor_tensor(a0a1c0v0[:], e_row[:].unsqueeze(1).to_broadcast([P, 4, 2, F]),
                                   w_row[:].unsqueeze(2).to_broadcast([P, 4, 2, F]),
                                   ALU.mult).then_inc(s["abc_made"], 1)
                pool.wait_ge(s["abc_made"], p + 1)

            def phi0(t, par, first=False):
                if not first:
                    pool.wait_ge(s["x0_turned"], (t - 1) * 4)
                pool.tensor_tensor(x0[:, par, :].rearrange("p (f g) -> p f g", g=F),
                                   a0a1c0v0[:, 0, par, :].unsqueeze(2).to_broadcast([P, F, F]),
                                   a0a1c0v0[:, 2, par, :].unsqueeze(1).to_broadcast([P, F, F]),
                                   ALU.mult).then_inc(s["phi0_made"], 1)

            def x0_values(t, par):
                pool.wait_ge(s["x0_scaled"], t + 1)
                v = x0[:, par, :].rearrange("p (f g) -> p f g", g=F)
                pool.tensor_tensor(v, v, a0a1c0v0[:, 3, par, :].unsqueeze(2).to_broadcast([P, F, F]),
                                   ALU.mult).then_inc(s["x0_made"], 1)

            def x1(m, i):
                pool.wait_ge(s["rec_kept"], m * 4 + (i // 2 + 1))
                pool.tensor_tensor(ex4[:, i, :, :], ex4[:, i, :, :],
                                   rec_field[:, i, :].unsqueeze(1).to_broadcast([P, FQ, G]),
                                   ALU.mult).then_inc(s["x1_by_pool"], 1)

            def turn(m, prev=True, main=True):
                if main:
                    weighted(m + 1)
                    phi0(m * 2 + 2, 0)
                if prev:
                    x1(m - 1, 4)
                    x1(m - 1, 5)
                if main:
                    x0_values(m * 2 + 2, 0)
                if prev:
                    x1(m - 1, 6)
                if main:
                    phi0(m * 2 + 3, 1)
                if prev:
                    x1(m - 1, 7)
                if main:
                    x1(m, 0)
                    x1(m, 1)
                    x0_values(m * 2 + 3, 1)
                    x1(m, 2)

            pool.wait_ge(s["loaded"], 16 * n_loads)
            weighted(0)
            phi0(0, 0, first=True)
            phi0(1, 1, first=True)
            x0_values(0, 0)
            x0_values(1, 1)
            turn(0, prev=False)
            with pool.Fori(1, PAIRS) as m:
                turn(m)
            turn(PAIRS, main=False)

        @block.vector
        def _(dve):
            class Steps:
                def __init__(self, base):
                    self.base, self.n = base, 0

                def mark(self, ins):
                    ins.then_inc(s["dve_step"], 1)
                    self.n += 1

                def wait(self):
                    dve.wait_ge(s["dve_step"], self.base + self.n)

                def link(self, ins):
                    self.mark(ins)
                    self.wait()

            def guard0(p, st, keep=True):
                if keep:
                    if not isinstance(p, int) or p > 1:
                        dve.wait_ge(s["cm_made"], p * 2 - 2)
                    st.link(dve.tensor_copy(hold[:], ends[:, :, 1, 1]))
                    dve.wait_ge(s["phi0_shifted"], p * 2)
                dve.wait_ge(s["abc_made"], p + 1)
                a = a0a1c0v0[:, 0:2, :, :]
                st.mark(dve.tensor_reduce(ends[:, 0, :, :], a, AX_X, ALU.max))
                st.link(dve.tensor_reduce(ends[:, 1, :, :], a, AX_X, ALU.min))
                c = a0a1c0v0[:, 2, :, :]
                st.mark(dve.tensor_tensor(mhi[:], c, ends[:, 0, 0, :].unsqueeze(2).to_broadcast([P, 2, F]), ALU.mult))
                st.link(dve.tensor_tensor(mlo[:], c, ends[:, 1, 0, :].unsqueeze(2).to_broadcast([P, 2, F]), ALU.mult))
                st.link(dve.tensor_tensor(m0[:], mhi[:], mlo[:], ALU.max))

            def shift0(t, par):
                dve.wait_ge(s["phi0_made"], t + 1)
                v = x0[:, par, :].rearrange("p (f g) -> p f g", g=F)
                dve.tensor_tensor(v, v, m0[:, par, :].unsqueeze(1).to_broadcast([P, F, F]),
                                  ALU.subtract).then_inc(s["phi0_shifted"], 1)

            def scale0(t, par, st):
                dve.wait_ge(s["exp0_made"], t + 1)
                if not isinstance(t, int) or t > 0:
                    dve.wait_ge(s["x0_scaled"], t)
                v = x0[:, par, :].rearrange("p (f g) -> p f g", g=F)
                st.link(dve.tensor_reduce(sum0[:], v.rearrange("p f g -> p g f"), AX_X, ALU.add))
                st.link(dve.reciprocal(rec0[:], sum0[:]))
                dve.tensor_tensor(v, v, rec0[:].unsqueeze(1).to_broadcast([P, F, F]),
                                  ALU.mult).then_inc(s["x0_scaled"], 1)

            def make_cm(t, par, st):
                hi, lo = (ends[:, 0, 1, 0:1], ends[:, 1, 1, 0:1]) if par == 0 else (hold[:, 0:1], hold[:, 1:2])
                dve.wait_ge(s["out0_kept"], t + 1)
                if not isinstance(t, int) or t > 0:
                    dve.wait_ge(s["cm_made"], t)
                st.link(dve.tensor_tensor(cm[:, par, 0, :], out0[:], wq1_row[:], ALU.mult))
                st.link(dve.tensor_scalar(low1[:], cm[:, par, 0, :], lo, None, ALU.mult))
                dve.scalar_tensor_tensor(out=cm[:, par, 1, :], in0=cm[:, par, 0, :], scalar=hi, in1=low1[:],
                                         op0=ALU.mult, op1=ALU.max).then_inc(s["cm_made"], 1)

            def phi1(m, i, prev):
                dve.wait_ge(s["m_kept"], m * 8 + i + 1)
                if prev:
                    dve.wait_ge(s["x_summed"], (m - 1) * 8 + i + 1)
                for f in range(FQ):
                    ins = dve.scalar_tensor_tensor(out=ex4[:, i, f, :], in0=pC[i % 2][:, 0:G],
                                                   scalar=a1[:, i, f:f + 1], in1=m_field[:, i % 2, :],
                                                   op0=ALU.mult, op1=ALU.subtract)
                ins.then_inc(s["phi1_made"], 1)

            def rec_1(t):
                dve.wait_ge(s["sums_made"], t + 1)
                if not isinstance(t, int) or t > 0:
                    dve.wait_ge(s["rec_spread"], t * 2)
                dve.reciprocal(rec1[:], pS[:, 0:G]).then_inc(s["rec_made"], 1)

            def x1(m, i):
                dve.wait_ge(s["rec_kept"], m * 4 + (i // 2 + 1))
                dve.tensor_tensor(ex4[:, i, :, :], ex4[:, i, :, :],
                                  rec_field[:, i, :].unsqueeze(1).to_broadcast([P, FQ, G]),
                                  ALU.mult).then_inc(s["x1_by_dve"], 1)

            def a_of(p):
                return dve.tensor_tensor(a1[:], e_field[:, bass.ds(p * 8, 8), :],
                                         w_field[:, 0, :].unsqueeze(1).to_broadcast([P, 8, FQ]), ALU.mult)

            def vsel_write(half, prev, m):
                if prev:
                    dve.wait_ge(s["x_summed"], (m - 1) * 8 + 4 * half + 4)
                b = slice(4 * half, 4 * half + 4)
                dve.tensor_tensor(vdiag[:, b, :, :], v1[:, b, :].unsqueeze(3).to_broadcast([P, 4, FQ, 4]),
                                  quad.unsqueeze(1).unsqueeze(1).to_broadcast([P, 4, FQ, 4]),
                                  ALU.mult).then_inc(s["vsel_hi" if half else "vsel_lo"], 1)

            def turn(m, prev=True, main=True):
                st = Steps(m * STEPS_TURN + STEPS_HEAD)
                if main:
                    phi1(m, 0, prev)
                    guard0(m + 1, st)
                    shift0(m * 2 + 2, 0)
                if prev:
                    rec_1(m * 2 - 1)
                if main:
                    phi1(m, 1, prev)
                if prev:
                    x1(m - 1, 3)
                if not main:
                    return
                phi1(m, 2, prev)
                make_cm(m * 2 + 1, 1, st)
                scale0(m * 2 + 2, 0, st)
                phi1(m, 3, prev)
                if prev:
                    dve.wait_ge(s["vsel_hi"], m)
                st.link(dve.tensor_tensor(v1[:], e_field[:, bass.ds(m * 8, 8), :],
                                          w_field[:, 1, :].unsqueeze(1).to_broadcast([P, 8, FQ]), ALU.mult))
                vsel_write(0, prev, m)
                phi1(m, 4, prev)
                shift0(m * 2 + 3, 1)
                rec_1(m * 2)
                phi1(m, 5, prev)
                phi1(m, 6, prev)
                make_cm(m * 2 + 2, 0, st)
                scale0(m * 2 + 3, 1, st)
                phi1(m, 7, prev)
                vsel_write(1, prev, m)
                dve.wait_ge(s["phi1_made"], m * 8 + 8)
                st.link(a_of(m + 1))
                assert st.n == STEPS_TURN

            dve.memset(vsel[:], 0.0).then_inc(s["zeroed"], 1)
            dve.memset(zeros[:], 0.0).then_inc(s["zeroed"], 1)
            dve.memset(e_field[:, B:, :], 0.0).then_inc(s["padded"], 1)
            dve.wait_ge(s["zeroed"], 2)
            dve.wait_ge(s["padded"], 1)
            dve.wait_ge(s["loaded"], 16 * n_loads)
            dve.wait_ge(s["e_kept"], 3 * CHUNKS)
            st = Steps(0)
            guard0(0, st, keep=False)
            shift0(0, 0)
            shift0(1, 1)
            scale0(0, 0, st)
            scale0(1, 1, st)
            make_cm(0, 0, st)
            st.link(a_of(0))
            assert st.n == STEPS_HEAD
            turn(0, prev=False)
            with dve.Fori(1, PAIRS) as m:
                turn(m)
            turn(PAIRS, main=False)

            with dve.Fori(0, BLOCKS) as blk:
                for u in range(1, 2 * FB, 2):
                    dve.wait_ge(s["xb_turned"], blk * (2 * FB) + u + 1)
                    dve.tensor_copy(xT[:, 1, :], pT[1][0:H, :]).then_inc(s["xT_dve"], 1)

        @block.scalar
        def _(act):
            for c in range(CHUNKS):
                for g in range(3):
                    q0, q1 = 4 * g, min(4 * g + 4, FQ)
                    act.wait_ge(s["e_turned"], 3 * c + g + 1)
                    nc.scalar.copy(e_field[:, c * P:(c + 1) * P, q0:q1].rearrange("p b q -> p q b"),
                                   pT[(3 * c + g) % 2][:, 0:(q1 - q0) * P].rearrange("p (q b) -> p q b", b=P)
                                   ).then_inc(s["e_kept"], 1)
            act.wait_ge(s["e_kept"], 3 * CHUNKS)
            act.wait_ge(s["padded"], 1)

            def e_rows(p, first=False):
                if not first:
                    act.wait_ge(s["abc_made"], p)
                src = e_field[:, bass.ds(p * 8, 8), :].rearrange("p (s i) q -> p s i q", i=NB)
                dst = e_row[:].rearrange("p s (q j) -> p s q j", j=FJ)
                for i in range(NB):
                    for j in range(FJ):
                        ins = nc.scalar.copy(dst[K * i:K * i + K, :, :, j], src[K * j:K * j + K, :, i, :])
                ins.then_inc(s["erow_made"], 1)

            def exp0(t, par):
                act.wait_ge(s["phi0_shifted"], t + 1)
                nc.scalar.activation(x0[:, par, :], x0[:, par, :], ACT.Exp).then_inc(s["exp0_made"], 1)

            def keep_x0T(t):
                for g in range(4):
                    act.wait_ge(s["x0_turned"], t * 4 + g + 1)
                    whole = [ch for ch in GROUPS[g] if ch < NCH - 1]
                    ins = nc.scalar.copy(x0T[:, whole[0]:whole[-1] + 1, :],
                                         pT[g % 2][:, 0:len(whole) * P].rearrange("p (c b) -> p c b", b=P))
                    if g == 3:
                        ins = nc.scalar.copy(x0T[0:TAIL, NCH - 1, :], pT[1][0:TAIL, P:2 * P])
                    ins.then_inc(s["x0T_kept"], 1)

            def keep_out0(t, first=False):
                act.wait_ge(s["out0_made"], t + 1)
                if not first:
                    act.wait_ge(s["cm_made"], t)
                nc.scalar.copy(out0[:], pO[:, 0:G]).then_inc(s["out0_kept"], 1)

            def keep_z0(t):
                act.wait_ge(s["z0_made"], t + 1)
                nc.scalar.copy(z0T[:, :, bass.ds(t * 4, 4)],
                               pO[0:H, 256:264].rearrange("p (h b) -> p h b", b=4)).then_inc(s["z0_kept"], 1)

            def keep_m(m, i):
                act.wait_ge(s["cm_spread"], m * 8 + i + 1)
                nc.scalar.copy(m_field[:, i % 2, :], pC[i % 2][:, G:2 * G]).then_inc(s["m_kept"], 1)

            def exp1(m, i):
                act.wait_ge(s["phi1_made"], m * 8 + i + 1)
                nc.scalar.activation(ex[:, i, :], ex[:, i, :], ACT.Exp).then_inc(s["exp1_made"], 1)

            def keep_rec(m, i2):
                act.wait_ge(s["rec_spread"], m * 4 + i2 + 1)
                nc.scalar.copy(rec_field[:, 2 * i2:2 * i2 + 2, :],
                               pR[:, 0:2 * G].rearrange("p (b g) -> p b g", g=G)).then_inc(s["rec_kept"], 1)

            def keep_xsum(m, first=False):
                act.wait_ge(s["x_summed"], m * 8 + 8)
                if not first:
                    act.wait_ge(s["spilled"], m * 16)
                nc.scalar.copy(xsum[:], pX[:, 0:500]).then_inc(s["xsum_kept"], 1)

            def turn(m, prev=True, main=True):
                if main:
                    exp1(m, 0)
                    keep_m(m, 2)
                    keep_x0T(m * 2 + 1)
                    keep_out0(m * 2 + 1)
                if prev:
                    keep_rec(m - 1, 2)
                    keep_rec(m - 1, 3)
                if main:
                    exp1(m, 1)
                    keep_m(m, 3)
                    exp0(m * 2 + 2, 0)
                    keep_z0(m * 2 + 1)
                    exp1(m, 2)
                    keep_m(m, 4)
                    exp1(m, 3)
                    keep_m(m, 5)
                    exp1(m, 4)
                    keep_m(m, 6)
                    keep_x0T(m * 2 + 2)
                    keep_out0(m * 2 + 2)
                    keep_rec(m, 0)
                    keep_rec(m, 1)
                    exp1(m, 5)
                    keep_m(m, 7)
                    exp0(m * 2 + 3, 1)
                    keep_z0(m * 2 + 2)
                    exp1(m, 6)
                    keep_m(m, 8)
                if prev:
                    if isinstance(m, int) and m == 1:
                        keep_xsum(0, first=True)
                    else:
                        keep_xsum(m - 1)
                if main:
                    e_rows(m + 2)
                    exp1(m, 7)
                    keep_m(m, 9)

            e_rows(0, first=True)
            exp0(0, 0)
            exp0(1, 1)
            keep_x0T(0)
            keep_out0(0, first=True)
            keep_z0(0)
            keep_m(0, 0)
            keep_m(0, 1)
            e_rows(1)
            turn(0, prev=False)
            turn(1)
            with act.Fori(2, PAIRS) as m:
                turn(m)
            turn(PAIRS, main=False)

            with act.Fori(0, BLOCKS) as blk:
                for u in range(0, 2 * FB, 2):
                    act.wait_ge(s["xb_turned"], blk * (2 * FB) + u + 1)
                    nc.scalar.copy(xT[:, 0, :], pT[0][0:H, :]).then_inc(s["xT_act"], 1)
            act.wait_ge(s["dense_turned"], 1)
            nc.scalar.copy(denseT[:], pT[0][0:NDENSE, :]).then_inc(s["dense_kept"], 1)
            act.wait_ge(s["z1_made"], 1)
            for h, z in enumerate((pS, pR)):
                nc.scalar.copy(z1T[:, h, :], z[0:H, :]).then_inc(s["z1_kept"], 1)
            for c in range(N1 // P):
                act.wait_ge(s["h1_made"], c + 1)
                nc.scalar.activation(h1T[:, c, :], pC[c % 2][:, :], ACT.Relu,
                                     bias=b1_sb[:, c:c + 1]).then_inc(s["h1_kept"], 1)
            for c in range(N2 // P):
                act.wait_ge(s["h2_made"], c + 1)
                nc.scalar.activation(h2T[:, c, :], pT[c][:, :], ACT.Relu,
                                     bias=b2_sb[:, c:c + 1]).then_inc(s["h2_kept"], 1)
            act.wait_ge(s["y_made"], 1)
            nc.scalar.copy(y_sb[:], pX[0:1, :]).then_inc(s["y_kept"], 1)

        @block.tensor
        def _(pe):
            pe.wait_ge(s["loaded"], 16 * n_loads)
            pe.wait_ge(s["zeroed"], 2)
            for c in range(CHUNKS):
                pe.wait_ge(gathered[c % 2], 16 * F * (c // 2 + 1))
                for g in range(3):
                    n = 3 * c + g
                    if n >= 2:
                        pe.wait_ge(s["e_kept"], n - 1)
                    for q in range(4 * g, min(4 * g + 4, FQ)):
                        ins = pe.transpose(pT[n % 2][:, (q - 4 * g) * P:(q - 4 * g + 1) * P],
                                           gath[:, c % 2, q * P:(q + 1) * P], ident)
                    ins.then_inc(s["e_turned"], 1)
            pe.wait_ge(s["e_kept"], 3 * CHUNKS)

            def out0_of(t, par, first=False):
                pe.wait_ge(s["x0_made"], t + 1)
                for g in range(4):
                    if g >= 2:
                        pe.wait_ge(s["x0T_kept"], t * 4 + g - 1)
                    for at, ch in enumerate(GROUPS[g]):
                        n = min(P, C0 - ch * P)
                        ins = pe.transpose(pT[g % 2][0:n, at * P:(at + 1) * P],
                                           x0[:, par, ch * P:ch * P + n], ident)
                    ins.then_inc(s["x0_turned"], 1)
                if not first:
                    pe.wait_ge(s["z0_kept"], t)
                for g, ch in ((g, ch) for g in range(4) for ch in GROUPS[g]):
                    n = min(P, C0 - ch * P)
                    if ch == GROUPS[g][0]:
                        pe.wait_ge(s["x0T_kept"], t * 4 + g + 1)
                    ins = pe.matmul(pO[:, 0:G], x0T[0:n, ch, :], cw0_sb[0:n, ch, :],
                                    start=(ch == 0), stop=(ch == NCH - 1))
                ins.then_inc(s["out0_made"], 1)

            def z0_of(t):
                pe.wait_ge(s["out0_kept"], t + 1)
                for h in range(2):
                    ins = pe.matmul(pO[0:H, 256 + 4 * h:260 + 4 * h], out0[:, h * H:(h + 1) * H], quad,
                                    start=True, stop=True)
                ins.then_inc(s["z0_made"], 1)

            def spread_cm(m, i, first=False):
                par = (i // 4) % 2
                pe.wait_ge(s["cm_made"], m * 2 + (i // 4 + 1))
                if not first:
                    pe.wait_ge(s["phi1_made"], m * 8 + i - 1)
                pe.matmul(pC[i % 2][:, 0:2 * G], spread[:, i % 4, :],
                          cm[:, par, :, :].rearrange("p a g -> p (a g)"),
                          start=True, stop=True).then_inc(s["cm_spread"], 1)

            def sums_of(m, half):
                t = m * 2 + half
                pe.wait_ge(s["exp1_made"], m * 8 + 4 * half + 4)
                if not isinstance(t, int) or t > 0:
                    pe.wait_ge(s["rec_made"], t)
                for f in range(FQ):
                    for i in range(NB):
                        ins = pe.matmul(pS[K * i:K * i + K, 0:G], delta, ex4[:, 4 * half + i, f, :],
                                        start=(f == 0), stop=(f == FQ - 1), skip_group_check=True)
                ins.then_inc(s["sums_made"], 1)

            def spread_rec(m, i2):
                pe.wait_ge(s["rec_made"], m * 2 + (i2 // 2 + 1))
                if not (isinstance(m, int) and m == 0 and i2 == 0):
                    pe.wait_ge(s["rec_kept"], m * 4 + i2)
                for b in range(2):
                    ins = pe.matmul(pR[:, b * G:(b + 1) * G], spread[:, (2 * i2 + b) % 4, :], rec1[:],
                                    start=True, stop=True)
                ins.then_inc(s["rec_spread"], 1)

            def xsum_of(m, i, first=False):
                if i == 3:
                    pe.wait_ge(s["x1_by_dve"], m + 1)
                else:
                    pe.wait_ge(s["x1_by_pool"], m * 7 + (i + 1 if i < 3 else i))
                pe.wait_ge(s["vsel_lo" if i < 4 else "vsel_hi"], m + 1)
                if i == 0 and not first:
                    pe.wait_ge(s["xsum_kept"], m)
                w = vflat[:, i * FQ * 32:(i + 1) * FQ * 32].rearrange("p (f c) -> p f c", c=32)
                for slot in range(3):
                    for c in range(4):
                        f = 4 * slot + c if slot < 2 else 8 + c // 2
                        g0, n = (0, G) if slot < 2 else (H * (c % 2), H)
                        ins = pe.matmul(pX[32 * c:32 * c + 32, slot * G:slot * G + n], w[:, f, :],
                                        ex4[:, i, f, g0:g0 + n], start=(i == 0 and slot == 0),
                                        stop=(i == 7 and slot == 2), skip_group_check=True)
                ins.then_inc(s["x_summed"], 1)

            def turn(m, prev=True, main=True):
                if prev:
                    sums_of(m - 1, 1)
                    xsum_of(m - 1, 1)
                if main:
                    spread_cm(m, 2)
                    out0_of(m * 2 + 1, 1)
                if prev:
                    spread_rec(m - 1, 2)
                    xsum_of(m - 1, 2)
                    spread_rec(m - 1, 3)
                if main:
                    spread_cm(m, 3)
                    z0_of(m * 2 + 1)
                if prev:
                    xsum_of(m - 1, 3)
                if main:
                    spread_cm(m, 4)
                if prev:
                    xsum_of(m - 1, 4)
                if main:
                    spread_cm(m, 5)
                    sums_of(m, 0)
                if prev:
                    xsum_of(m - 1, 5)
                if main:
                    spread_cm(m, 6)
                    out0_of(m * 2 + 2, 0)
                    spread_rec(m, 0)
                if prev:
                    xsum_of(m - 1, 6)
                if main:
                    spread_rec(m, 1)
                    spread_cm(m, 7)
                    z0_of(m * 2 + 2)
                if prev:
                    xsum_of(m - 1, 7)
                if main:
                    spread_cm(m, 8)
                    xsum_of(m, 0, first=not prev)
                    spread_cm(m, 9)

            out0_of(0, 0, first=True)
            z0_of(0)
            spread_cm(0, 0, first=True)
            spread_cm(0, 1, first=True)
            turn(0, prev=False)
            with pe.Fori(1, PAIRS) as m:
                turn(m)
            turn(PAIRS, main=False)

            pe.wait_ge(s["rec_kept"], 4 * PAIRS)
            pe.wait_ge(s["spilled"], 16 * PAIRS)
            for z in (pS, pR):
                pe.matmul(z[0:H, :], zeros[:], xT[:, 0, :],
                          start=True, stop=False, skip_group_check=True)
            with pe.Fori(0, BLOCKS // 2) as t2:
                for buf in range(2):
                    blk = t2 * 2 + buf
                    pe.wait_ge(xblk_loaded[buf], t2 * 16 + 16)
                    pe.wait_ge(cwblk_loaded[buf], t2 * 16 + 16)
                    for u in range(2 * FB):
                        for c in range(CHUNKS):
                            ins = pe.transpose(pT[u % 2][0:H, c * P:(c + 1) * P],
                                               xblk[:, buf, c, u * H:(u + 1) * H], ident)
                        ins.then_inc(s["xb_turned"], 1)
                        pe.wait_ge(s["xT_dve" if u % 2 else "xT_act"], blk * FB + (u // 2 + 1))
                        for h, z in enumerate((pS, pR)):
                            ins = pe.matmul(z[0:H, :], cwblk[:, buf, u, h * H:(h + 1) * H], xT[:, u % 2, :],
                                            start=False, stop=False, skip_group_check=True)
                        if u == 2 * FB - 1:
                            ins.then_inc(s["block_used"], 1)
            pe.wait_ge(s["loaded_top"], 16 * 7)
            for z in (pS, pR):
                ins = pe.matmul(z[0:H, :], zeros[:], xT[:, 0, :], start=False, stop=True, skip_group_check=True)
            ins.then_inc(s["z1_made"], 1)
            for c in range(CHUNKS):
                ins = pe.transpose(pT[0][0:NDENSE, c * P:(c + 1) * P], dense_sb[:, c, :], ident)
            ins.then_inc(s["dense_turned"], 1)
            pe.wait_ge(s["dense_kept"], 1)
            pe.wait_ge(s["z1_kept"], 2)
            zs = [z0T[:, 0, 0:B], z0T[:, 1, 0:B], z1T[:, 0, :], z1T[:, 1, :], denseT[:]]
            for c in range(N1 // P):
                if c >= 2:
                    pe.wait_ge(s["h1_kept"], c - 1)
                for r, z in enumerate(zs):
                    n = z.shape[0]
                    ins = pe.matmul(pC[c % 2][:, :], w1_sb[0:n, r, c * P:(c + 1) * P], z,
                                    start=(r == 0), stop=(r == 4))
                ins.then_inc(s["h1_made"], 1)
            pe.wait_ge(s["h1_kept"], 4)
            for c in range(N2 // P):
                for r in range(N1 // P):
                    ins = pe.matmul(pT[c][:, :], w2_sb[:, r, c * P:(c + 1) * P], h1T[:, r, :],
                                    start=(r == 0), stop=(r == N1 // P - 1))
                ins.then_inc(s["h2_made"], 1)
            pe.wait_ge(s["h2_kept"], 2)
            for r in range(N2 // P):
                ins = pe.matmul(pX[0:1, :], w3_sb[:, r:r + 1], h2T[:, r, :], start=(r == 0), stop=(r == 1))
            ins.then_inc(s["y_made"], 1)


def kernel(**inputs):
    import numpy as np
    import concourse.bacc as bacc
    from concourse.bass_utils import run_bass_kernel_spmd as run

    nc = bacc.Bacc("TRN2", target_bir_lowering=False, num_devices=1)
    arrays = {}

    def given(name, a):
        a = np.ascontiguousarray(a)
        arrays[name] = a
        return nc.dram_tensor(name, a.shape, mybir.dt.from_np(a.dtype), kind="ExternalInput").ap()

    def rows(w):
        return np.tile(np.asarray(w)[0].T, (NB, 1))

    def fields(w):
        return np.asarray(w)[0].reshape(FQ, FJ, K).transpose(1, 2, 0).reshape(P, FQ)

    r = inputs
    ids = given("ids_dram", r["ids"])
    tables = [given(f"tbl_{f}_dram", r[f"tbl_{f}"]) for f in range(F)]
    dense = given("dense_dram", r["dense_ctx"])
    wa = given("wa_dram", np.stack([rows(r["L0_rec_wk0"]), rows(r["L0_rec_wk1"]), rows(r["L0_rec_wq0"]),
                                    rows(r["L0_rec_wv0"])], axis=1))
    wq1 = given("wq1_dram", rows(r["L0_rec_wq1"]))
    wd = given("wd_dram", np.stack([fields(r["L0_rec_wk1"]), fields(r["L0_rec_wv1"])], axis=1))
    cw0 = given("cw0_dram", np.asarray(r["L0_rec_cw0"])[0])
    slices = np.asarray(r["L0_rec_cw1"])[0].reshape(F, 2, H, G)
    order = [sl for c in range(NB) for j in range(FJ)
             for sl in ((4 * c + j, 0), (4 * c + j, 1), (16 + 4 * c + j, 0), (16 + 4 * c + j, 1),
                        (32 + 4 * (c // 2) + j, c % 2))]
    cw1 = given("cw1_dram", slices[[f for f, _ in order], [h for _, h in order]].reshape(BLOCKS, 2 * FB, H, G))
    def columns(v):
        return np.asarray(v).reshape(-1, P).T

    w1, b1 = given("w1_dram", r["W_top1"]), given("b1_dram", columns(r["b_top1"]))
    w2, b2 = given("w2_dram", r["W_top2"]), given("b2_dram", columns(r["b_top2"]))
    w3 = given("w3_dram", columns(r["W_top3"]))
    p = np.arange(P)
    delta = (p[:, None] % K == np.arange(K)[None]).astype(np.float32)
    quad = (p[:, None] // K == np.arange(NB)[None]).astype(np.float32)
    spread = quad[:, :, None] * np.tile(delta, (1, NB))[:, None, :]
    consts = given("consts_dram", np.concatenate([np.eye(P, dtype=np.float32), delta, quad,
                                                  spread.reshape(P, NB * P)], axis=1))
    x_scratch = nc.dram_tensor("x_scratch", (NB, B, FJ, 5 * H), F32, kind="Internal").ap()
    out = nc.dram_tensor("y_dram", (B, 1), F32, kind="ExternalOutput").ap()
    cin_tower(nc, ids, tables, dense, wa, wq1, wd, cw0, cw1, w1, b1, w2, b2, w3, consts, x_scratch, out)
    res = run(nc, [arrays], core_ids=[0])
    return res.results[0]["y_dram"]
```

```python
from contextlib import ExitStack

import concourse.bass as bass
from concourse import mybir

ALU = mybir.AluOpType
ACT = mybir.ActivationFunctionType
F32 = mybir.dt.float32
I32 = mybir.dt.int32
AX_X = mybir.AxisListType.X

P = 128
B, F, K, G = 512, 40, 32, 200
NB = P // K
FJ, FQ = P // K, F * K // P
C0 = F * F
NCH = -(-C0 // P)
TAIL = C0 - (NCH - 1) * P
GROUPS = [range(0, 4), range(4, 8), range(8, 11), range(11, NCH)]
PAIRS = B // (2 * NB)
H = G // 2
NDENSE, N1, N2 = 16, 512, 256
CHUNKS = B // P
FB = 5
BLOCKS = F // FB
PLAIN = 3
SHARED = 7


def nth(i):
    return i + 1 if i < PLAIN else i


def counts(n):
    return not isinstance(n, int) or n > 0


def run_turns(engine, turn):
    turn(-2, (2,))
    turn(-1, (1, 2))
    turn(0, (0, 1, 2))
    turn(1, (-1, 0, 1, 2))
    with engine.Fori(2, PAIRS - 2) as m:
        turn(m, (-1, 0, 1, 2))
    turn(PAIRS - 2, (-1, 0, 1))
    turn(PAIRS - 1, (-1, 0))
    turn(PAIRS, (-1,))


def cin_tower(nc, ids, tables, dense, wa, wq1, wd, cw0, cw1, w1, b1, w2, b2, w3, consts, x_scratch, out):
    with ExitStack() as ctx:
        def sb(name, shape, dt=F32):
            return ctx.enter_context(nc.sbuf_tensor(name, shape, dt))

        def bank(name):
            return ctx.enter_context(nc.psum_tensor(name, [P, 512], F32))

        def sem(name):
            return ctx.enter_context(nc.semaphore(name))

        cst = sb("cst", [P, P + K + NB + NB * P])
        ident = cst[:, 0:P]
        delta = cst[:, P:P + K]
        quad = cst[:, P + K:P + K + NB]
        spread = cst[:, P + K + NB:].rearrange("p (i m) -> p i m", i=NB)
        idx = sb("idx", [P, CHUNKS, F], I32)
        gath = sb("gath", [P, 2, F * K])
        e_field = sb("e_field", [P, B, FQ])
        e_row = sb("e_row", [P, 2, F])
        w_row = sb("w_row", [P, 4, F])
        w_field = sb("w_field", [P, 2, FQ])
        wq1_row = sb("wq1_row", [P, G])
        a0a1c0v0 = sb("a0a1c0v0", [P, 4, 2, F])
        ends = sb("ends", [P, 2, 2, 2])
        hold = sb("hold", [P, 2])
        mlo = sb("mlo", [P, 2, F])
        mhi = sb("mhi", [P, 2, F])
        m0 = sb("m0", [P, 2, F])
        x0 = sb("x0", [P, 2, C0])
        sum0 = sb("sum0", [P, F])
        rec0 = sb("rec0", [P, F])
        x0T = sb("x0T", [P, NCH, P])
        cw0_sb = sb("cw0_sb", [P, NCH, G])
        out0 = sb("out0", [P, G])
        low1 = sb("low1", [P, G])
        cm = sb("cm", [P, 2, 2, G])
        m_field = sb("m_field", [P, 2, G])
        a1 = sb("a1", [P, 8, FQ])
        v1 = sb("v1", [P, 8, FQ])
        ex = sb("ex", [P, 8, FQ * G])
        rec1 = sb("rec1", [P, G])
        rec_field = sb("rec_field", [P, 8, G])
        vsel = sb("vsel", [P, 8 * (FQ * 32 + 4)])
        xsum = sb("xsum", [P, 500])
        z0T = sb("z0T", [H, 2, B])
        ex_flat = ex[:].rearrange("p b x -> p (b x)")
        xblk = ex_flat[:, 0:2 * CHUNKS * FB * G].rearrange("p (a c x) -> p a c x", a=2, c=CHUNKS)
        cwblk = ex_flat[0:H, 8 * FQ * G - 4 * FB * G:8 * FQ * G].rearrange("p (a u j) -> p a u j", a=2, j=G)
        xT = x0T[0:H, 0:8, :].rearrange("p (a c) b -> p a (c b)", a=2)
        zeros = sb("zeros", [H, H])
        z1T = sb("z1T", [H, 2, B])
        w1_sb = sb("w1_sb", [H, 5, N1])
        w2_sb = sb("w2_sb", [P, N1 // P, N2])
        w3_sb = sb("w3_sb", [P, N2 // P])
        b1_sb = sb("b1_sb", [P, N1 // P])
        b2_sb = sb("b2_sb", [P, N2 // P])
        dense_sb = sb("dense_sb", [P, CHUNKS, NDENSE])
        denseT = sb("denseT", [NDENSE, B])
        h1T = gath[:].rearrange("p a b -> p (a b)")[:, 0:4 * 512].rearrange("p (c b) -> p c b", b=B)
        h2T = x0[:].rearrange("p a b -> p (a b)")[:, 0:2 * 512].rearrange("p (c b) -> p c b", b=B)
        y_sb = sb("y_sb", [1, B])

        pT = [bank("pT0"), bank("pT1")]
        pO = bank("pO")
        pC = [bank("pC0"), bank("pC1")]
        pS = bank("pS")
        pR = bank("pR")
        pX = bank("pX")

        names = """loaded_idx loaded loaded_top gathered_even gathered_odd e_turned e_kept zeroed
            erow_made abc_made phi0_made phi0_shifted exp0_made x0_scaled x0_made
            x0_turned x0T_kept out0_made out0_kept z0_made z0_kept cm_made
            cm_spread m_kept a1_made products_made phi1_made exp1_made sums_made rec_made rec_spread rec_kept
            x1_by_pool x1_by_dve vsel_lo vsel_hi x_summed xsum_kept spilled
            hold_kept guard_step scale_step cm_step v1_made xblk_even xblk_odd cwblk_even cwblk_odd xb_turned xT_act xT_dve block_used z1_made z1_kept
            dense_turned dense_kept h1_made h1_kept h2_made h2_kept y_made y_kept y_stored"""
        s = {n: sem(n) for n in names.split()}

        gathered = [s["gathered_even"], s["gathered_odd"]]
        xblk_loaded = [s["xblk_even"], s["xblk_odd"]]
        cwblk_loaded = [s["cwblk_even"], s["cwblk_odd"]]

        vflat = vsel[:]
        vdiag = vflat.rearrange("p (b x) -> p b x", x=FQ * 32 + 4)[:, :, 0:FQ * 32].rearrange(
            "p b (f c) -> p b f c", c=32)[:, :, :, 0:4]
        ex4 = ex[:].rearrange("p b (f g) -> p b f g", g=G)
        n_loads = 6

        block = ctx.enter_context(nc.Block())

        @block.sync
        def _(sp):
            sp.dma_start(idx[:], ids.rearrange("(c p) f -> p c f", p=P)).then_inc(s["loaded_idx"], 16)
            for dst, src in ((cst[:], consts), (w_row[:], wa), (w_field[:], wd), (wq1_row[:], wq1),
                             (cw0_sb[:, 0:NCH - 1, :], cw0[0:(NCH - 1) * P, :].rearrange("(c p) j -> p c j", p=P)),
                             (cw0_sb[0:TAIL, NCH - 1, :], cw0[(NCH - 1) * P:, :])):
                sp.dma_start(dst, src).then_inc(s["loaded"], 16)
            for dst, src in ((w1_sb[:, 0:4, :], w1[0:4 * H, :].rearrange("(c p) j -> p c j", p=H)),
                             (w1_sb[0:NDENSE, 4, :], w1[4 * H:, :]),
                             (w2_sb[:], w2.rearrange("(c p) j -> p c j", p=P)),
                             (w3_sb[:], w3),
                             (b1_sb[:], b1),
                             (b2_sb[:], b2),
                             (dense_sb[:], dense.rearrange("(c p) j -> p c j", p=P))):
                sp.dma_start(dst, src).then_inc(s["loaded_top"], 16)

            def spill(m):
                sp.wait_ge(s["xsum_kept"], m + 1)
                sp.dma_start(x_scratch[:, bass.ds(m * 8, 8), :, :].rearrange("c b j x -> c (b j) x"),
                             xsum[:]).then_inc(s["spilled"], 16)

            with sp.Fori(0, PAIRS) as m:
                spill(m)
            sp.wait_ge(s["spilled"], 16 * PAIRS)

            def load_block(c, buf):
                sp.dma_start(xblk[:, buf, :, :],
                             x_scratch[bass.ds(c, 1), :, 2 * buf:2 * buf + 2, :].rearrange(
                                 "c (n p) j x -> p (c n) (j x)", p=P)).then_inc(xblk_loaded[buf], 16)
                sp.dma_start(cwblk[:, buf, :, :],
                             cw1[bass.ds(c * 2 + buf, 1), :, :, :].rearrange("c u p j -> p (c u) j")
                             ).then_inc(cwblk_loaded[buf], 16)

            load_block(0, 0)
            load_block(0, 1)
            with sp.Fori(1, BLOCKS // 2) as t:
                for buf in range(2):
                    sp.wait_ge(s["block_used"], t * 2 + buf - 1)
                    load_block(t, buf)
            sp.wait_ge(s["y_kept"], 1)
            sp.dma_start(out.rearrange("b o -> o b"), y_sb[:]).then_inc(s["y_stored"], 16)
            sp.wait_ge(s["y_stored"], 16)

        @block.gpsimd
        def _(pool):
            pool.wait_ge(s["loaded_idx"], 16)
            for c in range(CHUNKS):
                if c >= 2:
                    pool.wait_ge(s["e_turned"], 3 * (c - 1))
                for f in range(F):
                    pool.indirect_dma_start(
                        out=gath[:, c % 2, f * K:(f + 1) * K], out_offset=None, in_=tables[f],
                        in_offset=bass.IndirectOffsetOnAxis(ap=idx[:, c, f:f + 1], axis=0),
                    ).then_inc(gathered[c % 2], 16)

            def weighted(p):
                pool.wait_ge(s["erow_made"], p + 1)
                if counts(p):
                    pool.wait_ge(s["x0_made"], p * 2)
                pool.tensor_tensor(a0a1c0v0[:], e_row[:].unsqueeze(1).to_broadcast([P, 4, 2, F]),
                                   w_row[:].unsqueeze(2).to_broadcast([P, 4, 2, F]),
                                   ALU.mult).then_inc(s["abc_made"], 1)
                pool.wait_ge(s["abc_made"], p + 1)

            def phi0(p, h):
                if counts(p):
                    pool.wait_ge(s["x0_turned"], (p * 2 + h - 1) * 4)
                pool.tensor_tensor(x0[:, h, :].rearrange("p (f g) -> p f g", g=F),
                                   a0a1c0v0[:, 0, h, :].unsqueeze(2).to_broadcast([P, F, F]),
                                   a0a1c0v0[:, 2, h, :].unsqueeze(1).to_broadcast([P, F, F]),
                                   ALU.mult).then_inc(s["phi0_made"], 1)

            def x0_values(p, h):
                pool.wait_ge(s["x0_scaled"], p * 2 + h + 1)
                v = x0[:, h, :].rearrange("p (f g) -> p f g", g=F)
                pool.tensor_tensor(v, v, a0a1c0v0[:, 3, h, :].unsqueeze(2).to_broadcast([P, F, F]),
                                   ALU.mult).then_inc(s["x0_made"], 1)

            def x1(p, i):
                pool.wait_ge(s["rec_kept"], p * 4 + (i // 2 + 1))
                pool.tensor_tensor(ex4[:, i, :, :], ex4[:, i, :, :],
                                   rec_field[:, i, :].unsqueeze(1).to_broadcast([P, FQ, G]),
                                   ALU.mult).then_inc(s["x1_by_pool"], 1)

            def turn(m, live):
                if -1 in live:
                    x1(m - 1, 0)
                if 1 in live:
                    x0_values(m + 1, 0)
                if -1 in live:
                    x1(m - 1, 1)
                    x1(m - 1, 2)
                if 1 in live:
                    x0_values(m + 1, 1)
                if 2 in live:
                    weighted(m + 2)
                if -1 in live:
                    x1(m - 1, 4)
                    x1(m - 1, 5)
                if 2 in live:
                    phi0(m + 2, 0)
                if -1 in live:
                    x1(m - 1, 6)
                    x1(m - 1, 7)
                if 2 in live:
                    phi0(m + 2, 1)

            pool.wait_ge(s["loaded"], 16 * n_loads)
            run_turns(pool, turn)

        @block.vector
        def _(dve):
            def guard0(p):
                if counts(p):
                    dve.wait_ge(s["cm_made"], p * 2 - 1)
                    dve.tensor_copy(hold[:], ends[:, :, 1, 1]).then_inc(s["hold_kept"], 1)
                    dve.wait_ge(s["hold_kept"], p)
                    dve.wait_ge(s["phi0_shifted"], p * 2)
                dve.wait_ge(s["abc_made"], p + 1)
                a = a0a1c0v0[:, 0:2, :, :]
                dve.tensor_reduce(ends[:, 0, :, :], a, AX_X, ALU.max).then_inc(s["guard_step"], 1)
                dve.tensor_reduce(ends[:, 1, :, :], a, AX_X, ALU.min).then_inc(s["guard_step"], 1)
                dve.wait_ge(s["guard_step"], p * 5 + 2)
                c = a0a1c0v0[:, 2, :, :]
                dve.tensor_tensor(mhi[:], c, ends[:, 0, 0, :].unsqueeze(2).to_broadcast([P, 2, F]),
                                  ALU.mult).then_inc(s["guard_step"], 1)
                dve.tensor_tensor(mlo[:], c, ends[:, 1, 0, :].unsqueeze(2).to_broadcast([P, 2, F]),
                                  ALU.mult).then_inc(s["guard_step"], 1)
                dve.wait_ge(s["guard_step"], p * 5 + 4)
                dve.tensor_tensor(m0[:], mhi[:], mlo[:], ALU.max).then_inc(s["guard_step"], 1)

            def shift0(p, h):
                dve.wait_ge(s["phi0_made"], p * 2 + h + 1)
                dve.wait_ge(s["guard_step"], p * 5 + 5)
                v = x0[:, h, :].rearrange("p (f g) -> p f g", g=F)
                dve.tensor_tensor(v, v, m0[:, h, :].unsqueeze(1).to_broadcast([P, F, F]),
                                  ALU.subtract).then_inc(s["phi0_shifted"], 1)

            def scale0(p, h):
                t = p * 2 + h
                dve.wait_ge(s["exp0_made"], t + 1)
                if counts(t):
                    dve.wait_ge(s["x0_scaled"], t)
                v = x0[:, h, :].rearrange("p (f g) -> p f g", g=F)
                dve.tensor_reduce(sum0[:], v.rearrange("p f g -> p g f"), AX_X, ALU.add).then_inc(s["scale_step"], 1)
                dve.wait_ge(s["scale_step"], t * 2 + 1)
                dve.reciprocal(rec0[:], sum0[:]).then_inc(s["scale_step"], 1)
                dve.wait_ge(s["scale_step"], t * 2 + 2)
                dve.tensor_tensor(v, v, rec0[:].unsqueeze(1).to_broadcast([P, F, F]),
                                  ALU.mult).then_inc(s["x0_scaled"], 1)

            def make_cm(p, h, last=False):
                t = p * 2 + h
                hi, lo = (hold[:, 0:1], hold[:, 1:2]) if h and not last else (ends[:, 0, 1, h:h + 1],
                                                                             ends[:, 1, 1, h:h + 1])
                dve.wait_ge(s["out0_kept"], t + 1)
                if counts(t):
                    dve.wait_ge(s["cm_made"], t)
                if counts(p):
                    dve.wait_ge(s["cm_spread"], p * 8 - 4 + 4 * h)
                dve.tensor_tensor(cm[:, h, 0, :], out0[:], wq1_row[:], ALU.mult).then_inc(s["cm_step"], 1)
                dve.wait_ge(s["cm_step"], t * 2 + 1)
                dve.tensor_scalar(low1[:], cm[:, h, 0, :], lo, None, ALU.mult).then_inc(s["cm_step"], 1)
                dve.wait_ge(s["cm_step"], t * 2 + 2)
                dve.scalar_tensor_tensor(out=cm[:, h, 1, :], in0=cm[:, h, 0, :], scalar=hi, in1=low1[:],
                                         op0=ALU.mult, op1=ALU.max).then_inc(s["cm_made"], 1)

            def phi1(p, i):
                if i == PLAIN:
                    dve.wait_ge(s["m_kept"], p * 8 + i + 1)
                    dve.wait_ge(s["a1_made"], p + 1)
                    if counts(p):
                        dve.wait_ge(s["x_summed"], (p - 1) * 8 + i + 1)
                    for f in range(FQ):
                        ins = dve.scalar_tensor_tensor(out=ex4[:, i, f, :], in0=pC[i % 2][:, 0:G],
                                                       scalar=a1[:, i, f:f + 1], in1=m_field[:, i % 2, :],
                                                       op0=ALU.mult, op1=ALU.subtract)
                else:
                    dve.wait_ge(s["products_made"], p * SHARED + nth(i))
                    ins = dve.tensor_tensor(ex4[:, i, :, :], ex4[:, i, :, :],
                                            m_field[:, i % 2, :].unsqueeze(1).to_broadcast([P, FQ, G]),
                                            ALU.subtract)
                ins.then_inc(s["phi1_made"], 1)

            def rec_1(t):
                dve.wait_ge(s["sums_made"], t + 1)
                if counts(t):
                    dve.wait_ge(s["rec_spread"], t * 2)
                dve.reciprocal(rec1[:], pS[:, 0:G]).then_inc(s["rec_made"], 1)

            def x1(p):
                dve.wait_ge(s["rec_kept"], p * 4 + (PLAIN // 2 + 1))
                dve.tensor_tensor(ex4[:, PLAIN, :, :], ex4[:, PLAIN, :, :],
                                  rec_field[:, PLAIN, :].unsqueeze(1).to_broadcast([P, FQ, G]),
                                  ALU.mult).then_inc(s["x1_by_dve"], 1)

            def a1_of(p):
                if counts(p):
                    dve.wait_ge(s["products_made"], p * SHARED)
                    dve.wait_ge(s["phi1_made"], (p - 1) * 8 + PLAIN + 1)
                dve.tensor_tensor(a1[:], e_field[:, bass.ds(p * 8, 8), :],
                                  w_field[:, 0, :].unsqueeze(1).to_broadcast([P, 8, FQ]),
                                  ALU.mult).then_inc(s["a1_made"], 1)

            def v1_of(p):
                if counts(p):
                    dve.wait_ge(s["vsel_hi"], p)
                dve.tensor_tensor(v1[:], e_field[:, bass.ds(p * 8, 8), :],
                                  w_field[:, 1, :].unsqueeze(1).to_broadcast([P, 8, FQ]),
                                  ALU.mult).then_inc(s["v1_made"], 1)

            def vsel_write(p, half):
                dve.wait_ge(s["v1_made"], p + 1)
                if counts(p):
                    dve.wait_ge(s["x_summed"], (p - 1) * 8 + 4 * half + 4)
                b = slice(4 * half, 4 * half + 4)
                dve.tensor_tensor(vdiag[:, b, :, :], v1[:, b, :].unsqueeze(3).to_broadcast([P, 4, FQ, 4]),
                                  quad.unsqueeze(1).unsqueeze(1).to_broadcast([P, 4, FQ, 4]),
                                  ALU.mult).then_inc(s["vsel_hi" if half else "vsel_lo"], 1)

            def turn(m, live):
                if 1 in live:
                    shift0(m + 1, 1)
                if -1 in live:
                    x1(m - 1)
                if 0 in live:
                    a1_of(m)
                if 1 in live:
                    scale0(m + 1, 1)
                if -1 in live:
                    rec_1(m * 2 - 1)
                if 0 in live:
                    phi1(m, 0)
                    make_cm(m, 1, last=2 not in live and 1 not in live)
                if -1 in live:
                    vsel_write(m - 1, 1)
                if 0 in live:
                    phi1(m, 1)
                    phi1(m, 2)
                    phi1(m, 3)
                if 1 in live:
                    make_cm(m + 1, 0)
                if 0 in live:
                    v1_of(m)
                    vsel_write(m, 0)
                if 2 in live:
                    guard0(m + 2)
                    shift0(m + 2, 0)
                if 0 in live:
                    phi1(m, 4)
                    rec_1(m * 2)
                    phi1(m, 5)
                if 2 in live:
                    scale0(m + 2, 0)
                if 0 in live:
                    phi1(m, 6)
                    phi1(m, 7)

            dve.memset(vsel[:], 0.0).then_inc(s["zeroed"], 1)
            dve.memset(zeros[:], 0.0).then_inc(s["zeroed"], 1)
            dve.wait_ge(s["zeroed"], 2)
            dve.wait_ge(s["loaded"], 16 * n_loads)
            dve.wait_ge(s["e_kept"], 3 * CHUNKS)
            run_turns(dve, turn)

            with dve.Fori(0, BLOCKS) as blk:
                for u in range(1, 2 * FB, 2):
                    dve.wait_ge(s["xb_turned"], blk * (2 * FB) + u + 1)
                    dve.tensor_copy(xT[:, 1, :], pT[1][0:H, :]).then_inc(s["xT_dve"], 1)

        @block.scalar
        def _(act):
            for c in range(CHUNKS):
                for g in range(3):
                    q0, q1 = 4 * g, min(4 * g + 4, FQ)
                    act.wait_ge(s["e_turned"], 3 * c + g + 1)
                    nc.scalar.copy(e_field[:, c * P:(c + 1) * P, q0:q1].rearrange("p b q -> p q b"),
                                   pT[(3 * c + g) % 2][:, 0:(q1 - q0) * P].rearrange("p (q b) -> p q b", b=P)
                                   ).then_inc(s["e_kept"], 1)
            act.wait_ge(s["e_kept"], 3 * CHUNKS)

            def e_rows(p):
                if counts(p):
                    act.wait_ge(s["abc_made"], p)
                src = e_field[:, bass.ds(p * 8, 8), :].rearrange("p (s i) q -> p s i q", i=NB)
                dst = e_row[:].rearrange("p s (q j) -> p s q j", j=FJ)
                for i in range(NB):
                    for j in range(FJ):
                        ins = nc.scalar.copy(dst[K * i:K * i + K, :, :, j], src[K * j:K * j + K, :, i, :])
                ins.then_inc(s["erow_made"], 1)

            def exp0(p, h):
                act.wait_ge(s["phi0_shifted"], p * 2 + h + 1)
                nc.scalar.activation(x0[:, h, :], x0[:, h, :], ACT.Exp).then_inc(s["exp0_made"], 1)

            def keep_x0T(p, h, g):
                act.wait_ge(s["x0_turned"], (p * 2 + h) * 4 + g + 1)
                whole = [ch for ch in GROUPS[g] if ch < NCH - 1]
                ins = nc.scalar.copy(x0T[:, whole[0]:whole[-1] + 1, :],
                                     pT[g % 2][:, 0:len(whole) * P].rearrange("p (c b) -> p c b", b=P))
                if g == 3:
                    ins = nc.scalar.copy(x0T[0:TAIL, NCH - 1, :], pT[1][0:TAIL, P:2 * P])
                ins.then_inc(s["x0T_kept"], 1)

            def keep_out0(p, h):
                t = p * 2 + h
                act.wait_ge(s["out0_made"], t + 1)
                if counts(t):
                    act.wait_ge(s["cm_made"], t)
                nc.scalar.copy(out0[:], pO[:, 0:G]).then_inc(s["out0_kept"], 1)

            def keep_z0(p, h):
                t = p * 2 + h
                act.wait_ge(s["z0_made"], t + 1)
                nc.scalar.copy(z0T[:, :, bass.ds(t * 4, 4)],
                               pO[0:H, 256:264].rearrange("p (h b) -> p h b", b=4)).then_inc(s["z0_kept"], 1)

            def keep_m(p, i):
                act.wait_ge(s["cm_spread"], p * 8 + i + 1)
                n = p * 8 + i - 1
                if counts(n):
                    act.wait_ge(s["phi1_made"], n)
                nc.scalar.copy(m_field[:, i % 2, :], pC[i % 2][:, G:2 * G]).then_inc(s["m_kept"], 1)

            def products(p, i):
                act.wait_ge(s["a1_made"], p + 1)
                if counts(p):
                    act.wait_ge(s["x_summed"], (p - 1) * 8 + i + 1)
                for f in range(FQ):
                    ins = nc.scalar.activation(ex4[:, i, f, :], pC[i % 2][:, 0:G], ACT.Copy,
                                               scale=a1[:, i, f:f + 1])
                ins.then_inc(s["products_made"], 1)

            def exp1(p, i):
                act.wait_ge(s["phi1_made"], p * 8 + i + 1)
                nc.scalar.activation(ex[:, i, :], ex[:, i, :], ACT.Exp).then_inc(s["exp1_made"], 1)

            def keep_rec(p, i2):
                act.wait_ge(s["rec_spread"], p * 4 + i2 + 1)
                nc.scalar.copy(rec_field[:, 2 * i2:2 * i2 + 2, :],
                               pR[:, 0:2 * G].rearrange("p (b g) -> p b g", g=G)).then_inc(s["rec_kept"], 1)

            def keep_xsum(p):
                act.wait_ge(s["x_summed"], p * 8 + 8)
                if counts(p):
                    act.wait_ge(s["spilled"], p * 16)
                nc.scalar.copy(xsum[:], pX[:, 0:500]).then_inc(s["xsum_kept"], 1)

            def turn(m, live):
                if -1 in live:
                    exp1(m - 1, 6)
                    keep_rec(m - 1, 1)
                    exp1(m - 1, 7)
                if 1 in live:
                    exp0(m + 1, 1)
                    keep_x0T(m + 1, 0, 0)
                if 2 in live:
                    e_rows(m + 2)
                if 0 in live:
                    keep_out0(m, 1)
                    keep_m(m, 0)
                if 1 in live:
                    keep_x0T(m + 1, 0, 1)
                if 0 in live:
                    products(m, 0)
                    keep_z0(m, 1)
                    keep_m(m, 1)
                    products(m, 1)
                if 1 in live:
                    keep_x0T(m + 1, 0, 2)
                if -1 in live:
                    keep_rec(m - 1, 2)
                if 1 in live:
                    keep_x0T(m + 1, 0, 3)
                if 0 in live:
                    keep_m(m, 2)
                    products(m, 2)
                    exp1(m, 0)
                    keep_m(m, 3)
                    exp1(m, 1)
                    exp1(m, 2)
                if 1 in live:
                    keep_out0(m + 1, 0)
                    keep_x0T(m + 1, 1, 0)
                if -1 in live:
                    keep_rec(m - 1, 3)
                if 0 in live:
                    keep_m(m, 4)
                    exp1(m, 3)
                    keep_m(m, 5)
                if 1 in live:
                    keep_x0T(m + 1, 1, 1)
                if 0 in live:
                    products(m, 4)
                    products(m, 5)
                if 2 in live:
                    exp0(m + 2, 0)
                if 0 in live:
                    exp1(m, 4)
                    keep_m(m, 6)
                    products(m, 6)
                    keep_rec(m, 0)
                if 1 in live:
                    keep_x0T(m + 1, 1, 2)
                    keep_z0(m + 1, 0)
                if 0 in live:
                    keep_m(m, 7)
                if 1 in live:
                    keep_x0T(m + 1, 1, 3)
                if 0 in live:
                    products(m, 7)
                if -1 in live:
                    keep_xsum(m - 1)
                if 0 in live:
                    exp1(m, 5)

            run_turns(act, turn)

            with act.Fori(0, BLOCKS) as blk:
                for u in range(0, 2 * FB, 2):
                    act.wait_ge(s["xb_turned"], blk * (2 * FB) + u + 1)
                    nc.scalar.copy(xT[:, 0, :], pT[0][0:H, :]).then_inc(s["xT_act"], 1)
            act.wait_ge(s["dense_turned"], 1)
            nc.scalar.copy(denseT[:], pT[0][0:NDENSE, :]).then_inc(s["dense_kept"], 1)
            act.wait_ge(s["z1_made"], 1)
            for h, z in enumerate((pS, pR)):
                nc.scalar.copy(z1T[:, h, :], z[0:H, :]).then_inc(s["z1_kept"], 1)
            for c in range(N1 // P):
                act.wait_ge(s["h1_made"], c + 1)
                nc.scalar.activation(h1T[:, c, :], pC[c % 2][:, :], ACT.Relu,
                                     bias=b1_sb[:, c:c + 1]).then_inc(s["h1_kept"], 1)
            for c in range(N2 // P):
                act.wait_ge(s["h2_made"], c + 1)
                nc.scalar.activation(h2T[:, c, :], pT[c][:, :], ACT.Relu,
                                     bias=b2_sb[:, c:c + 1]).then_inc(s["h2_kept"], 1)
            act.wait_ge(s["y_made"], 1)
            nc.scalar.copy(y_sb[:], pX[0:1, :]).then_inc(s["y_kept"], 1)

        @block.tensor
        def _(pe):
            pe.wait_ge(s["loaded"], 16 * n_loads)
            pe.wait_ge(s["zeroed"], 2)
            for c in range(CHUNKS):
                pe.wait_ge(gathered[c % 2], 16 * F * (c // 2 + 1))
                for g in range(3):
                    n = 3 * c + g
                    if n >= 2:
                        pe.wait_ge(s["e_kept"], n - 1)
                    for q in range(4 * g, min(4 * g + 4, FQ)):
                        ins = pe.transpose(pT[n % 2][:, (q - 4 * g) * P:(q - 4 * g + 1) * P],
                                           gath[:, c % 2, q * P:(q + 1) * P], ident)
                    ins.then_inc(s["e_turned"], 1)
            pe.wait_ge(s["e_kept"], 3 * CHUNKS)

            def turn_x0(p, h, g):
                t = p * 2 + h
                pe.wait_ge(s["x0_made"], t + 1)
                n = t * 4 + g - 1
                if counts(n):
                    pe.wait_ge(s["x0T_kept"], n)
                for at, ch in enumerate(GROUPS[g]):
                    n = min(P, C0 - ch * P)
                    ins = pe.transpose(pT[g % 2][0:n, at * P:(at + 1) * P], x0[:, h, ch * P:ch * P + n], ident)
                ins.then_inc(s["x0_turned"], 1)

            def out0_of(p, h, g):
                t = p * 2 + h
                if g == 0 and counts(t):
                    pe.wait_ge(s["z0_kept"], t)
                pe.wait_ge(s["x0T_kept"], t * 4 + g + 1)
                for ch in GROUPS[g]:
                    n = min(P, C0 - ch * P)
                    ins = pe.matmul(pO[:, 0:G], x0T[0:n, ch, :], cw0_sb[0:n, ch, :],
                                    start=(ch == 0), stop=(ch == NCH - 1))
                if g == 3:
                    ins.then_inc(s["out0_made"], 1)

            def z0_of(p, h):
                pe.wait_ge(s["out0_kept"], p * 2 + h + 1)
                for j in range(2):
                    ins = pe.matmul(pO[0:H, 256 + 4 * j:260 + 4 * j], out0[:, j * H:(j + 1) * H], quad,
                                    start=True, stop=True)
                ins.then_inc(s["z0_made"], 1)

            def spread_cm(p, i):
                pe.wait_ge(s["cm_made"], p * 2 + (i // 4 + 1))
                n = p * SHARED + (nth(i - 2) if i >= 2 else i - 1)
                if i - 2 == PLAIN:
                    pe.wait_ge(s["phi1_made"], p * 8 + PLAIN + 1)
                elif counts(n):
                    pe.wait_ge(s["products_made"], n)
                pe.matmul(pC[i % 2][:, 0:2 * G], spread[:, i % 4, :],
                          cm[:, i // 4, :, :].rearrange("p a g -> p (a g)"),
                          start=True, stop=True).then_inc(s["cm_spread"], 1)

            def sums_of(p, half):
                t = p * 2 + half
                pe.wait_ge(s["exp1_made"], p * 8 + 4 * half + 4)
                if counts(t):
                    pe.wait_ge(s["rec_made"], t)
                for f in range(FQ):
                    for i in range(NB):
                        ins = pe.matmul(pS[K * i:K * i + K, 0:G], delta, ex4[:, 4 * half + i, f, :],
                                        start=(f == 0), stop=(f == FQ - 1), skip_group_check=True)
                ins.then_inc(s["sums_made"], 1)

            def spread_rec(p, i2):
                pe.wait_ge(s["rec_made"], p * 2 + (i2 // 2 + 1))
                n = p * 4 + i2
                if counts(n):
                    pe.wait_ge(s["rec_kept"], n)
                for b in range(2):
                    ins = pe.matmul(pR[:, b * G:(b + 1) * G], spread[:, (2 * i2 + b) % 4, :], rec1[:],
                                    start=True, stop=True)
                ins.then_inc(s["rec_spread"], 1)

            def xsum_of(p, i):
                if i == PLAIN:
                    pe.wait_ge(s["x1_by_dve"], p + 1)
                else:
                    pe.wait_ge(s["x1_by_pool"], p * SHARED + nth(i))
                pe.wait_ge(s["vsel_lo" if i < 4 else "vsel_hi"], p + 1)
                if i == 0 and counts(p):
                    pe.wait_ge(s["xsum_kept"], p)
                w = vflat[:, i * FQ * 32:(i + 1) * FQ * 32].rearrange("p (f c) -> p f c", c=32)
                for slot in range(3):
                    for c in range(4):
                        f = 4 * slot + c if slot < 2 else 8 + c // 2
                        g0, n = (0, G) if slot < 2 else (H * (c % 2), H)
                        ins = pe.matmul(pX[32 * c:32 * c + 32, slot * G:slot * G + n], w[:, f, :],
                                        ex4[:, i, f, g0:g0 + n], start=(i == 0 and slot == 0),
                                        stop=(i == 7 and slot == 2), skip_group_check=True)
                ins.then_inc(s["x_summed"], 1)

            def turn(m, live):
                if 0 in live:
                    out0_of(m, 1, 0)
                    spread_cm(m, 0)
                    out0_of(m, 1, 1)
                    out0_of(m, 1, 2)
                if -1 in live:
                    spread_rec(m - 1, 1)
                if 0 in live:
                    out0_of(m, 1, 3)
                if -1 in live:
                    xsum_of(m - 1, 0)
                if 0 in live:
                    spread_cm(m, 1)
                if 1 in live:
                    turn_x0(m + 1, 0, 0)
                    turn_x0(m + 1, 0, 1)
                if -1 in live:
                    sums_of(m - 1, 1)
                if 0 in live:
                    z0_of(m, 1)
                if -1 in live:
                    xsum_of(m - 1, 1)
                if 1 in live:
                    turn_x0(m + 1, 0, 2)
                if 0 in live:
                    spread_cm(m, 2)
                if 1 in live:
                    turn_x0(m + 1, 0, 3)
                if -1 in live:
                    spread_rec(m - 1, 2)
                    xsum_of(m - 1, 2)
                if 0 in live:
                    spread_cm(m, 3)
                if 1 in live:
                    out0_of(m + 1, 0, 0)
                if -1 in live:
                    xsum_of(m - 1, 3)
                if 1 in live:
                    turn_x0(m + 1, 1, 0)
                    out0_of(m + 1, 0, 1)
                    out0_of(m + 1, 0, 2)
                    out0_of(m + 1, 0, 3)
                if 0 in live:
                    spread_cm(m, 4)
                if 1 in live:
                    turn_x0(m + 1, 1, 1)
                if -1 in live:
                    spread_rec(m - 1, 3)
                    xsum_of(m - 1, 4)
                if 0 in live:
                    spread_cm(m, 5)
                if 1 in live:
                    turn_x0(m + 1, 1, 2)
                if -1 in live:
                    xsum_of(m - 1, 5)
                if 0 in live:
                    sums_of(m, 0)
                    spread_cm(m, 6)
                if 1 in live:
                    z0_of(m + 1, 0)
                if -1 in live:
                    xsum_of(m - 1, 6)
                if 0 in live:
                    spread_cm(m, 7)
                    spread_rec(m, 0)
                if 1 in live:
                    turn_x0(m + 1, 1, 3)
                if -1 in live:
                    xsum_of(m - 1, 7)

            run_turns(pe, turn)

            pe.wait_ge(s["rec_kept"], 4 * PAIRS)
            pe.wait_ge(s["spilled"], 16 * PAIRS)
            for z in (pS, pR):
                pe.matmul(z[0:H, :], zeros[:], xT[:, 0, :],
                          start=True, stop=False, skip_group_check=True)
            with pe.Fori(0, BLOCKS // 2) as t2:
                for buf in range(2):
                    blk = t2 * 2 + buf
                    pe.wait_ge(xblk_loaded[buf], t2 * 16 + 16)
                    pe.wait_ge(cwblk_loaded[buf], t2 * 16 + 16)
                    for u in range(2 * FB):
                        for c in range(CHUNKS):
                            ins = pe.transpose(pT[u % 2][0:H, c * P:(c + 1) * P],
                                               xblk[:, buf, c, u * H:(u + 1) * H], ident)
                        ins.then_inc(s["xb_turned"], 1)
                        pe.wait_ge(s["xT_dve" if u % 2 else "xT_act"], blk * FB + (u // 2 + 1))
                        for h, z in enumerate((pS, pR)):
                            ins = pe.matmul(z[0:H, :], cwblk[:, buf, u, h * H:(h + 1) * H], xT[:, u % 2, :],
                                            start=False, stop=False, skip_group_check=True)
                        if u == 2 * FB - 1:
                            ins.then_inc(s["block_used"], 1)
            pe.wait_ge(s["loaded_top"], 16 * 7)
            for z in (pS, pR):
                ins = pe.matmul(z[0:H, :], zeros[:], xT[:, 0, :], start=False, stop=True, skip_group_check=True)
            ins.then_inc(s["z1_made"], 1)
            for c in range(CHUNKS):
                ins = pe.transpose(pT[0][0:NDENSE, c * P:(c + 1) * P], dense_sb[:, c, :], ident)
            ins.then_inc(s["dense_turned"], 1)
            pe.wait_ge(s["dense_kept"], 1)
            pe.wait_ge(s["z1_kept"], 2)
            zs = [z0T[:, 0, 0:B], z0T[:, 1, 0:B], z1T[:, 0, :], z1T[:, 1, :], denseT[:]]
            for c in range(N1 // P):
                if c >= 2:
                    pe.wait_ge(s["h1_kept"], c - 1)
                for r, z in enumerate(zs):
                    n = z.shape[0]
                    ins = pe.matmul(pC[c % 2][:, :], w1_sb[0:n, r, c * P:(c + 1) * P], z,
                                    start=(r == 0), stop=(r == 4))
                ins.then_inc(s["h1_made"], 1)
            pe.wait_ge(s["h1_kept"], 4)
            for c in range(N2 // P):
                for r in range(N1 // P):
                    ins = pe.matmul(pT[c][:, :], w2_sb[:, r, c * P:(c + 1) * P], h1T[:, r, :],
                                    start=(r == 0), stop=(r == N1 // P - 1))
                ins.then_inc(s["h2_made"], 1)
            pe.wait_ge(s["h2_kept"], 2)
            for r in range(N2 // P):
                ins = pe.matmul(pX[0:1, :], w3_sb[:, r:r + 1], h2T[:, r, :], start=(r == 0), stop=(r == 1))
            ins.then_inc(s["y_made"], 1)


def kernel(**inputs):
    import numpy as np
    import concourse.bacc as bacc
    from concourse.bass_utils import run_bass_kernel_spmd as run

    nc = bacc.Bacc("TRN2", target_bir_lowering=False, num_devices=1)
    arrays = {}

    def given(name, a):
        a = np.ascontiguousarray(a)
        arrays[name] = a
        return nc.dram_tensor(name, a.shape, mybir.dt.from_np(a.dtype), kind="ExternalInput").ap()

    def rows(w):
        return np.tile(np.asarray(w)[0].T, (NB, 1))

    def fields(w):
        return np.asarray(w)[0].reshape(FQ, FJ, K).transpose(1, 2, 0).reshape(P, FQ)

    r = inputs
    ids = given("ids_dram", r["ids"])
    tables = [given(f"tbl_{f}_dram", r[f"tbl_{f}"]) for f in range(F)]
    dense = given("dense_dram", r["dense_ctx"])
    wa = given("wa_dram", np.stack([rows(r["L0_rec_wk0"]), rows(r["L0_rec_wk1"]), rows(r["L0_rec_wq0"]),
                                    rows(r["L0_rec_wv0"])], axis=1))
    wq1 = given("wq1_dram", rows(r["L0_rec_wq1"]))
    wd = given("wd_dram", np.stack([fields(r["L0_rec_wk1"]), fields(r["L0_rec_wv1"])], axis=1))
    cw0 = given("cw0_dram", np.asarray(r["L0_rec_cw0"])[0])
    slices = np.asarray(r["L0_rec_cw1"])[0].reshape(F, 2, H, G)
    order = [sl for c in range(NB) for j in range(FJ)
             for sl in ((4 * c + j, 0), (4 * c + j, 1), (16 + 4 * c + j, 0), (16 + 4 * c + j, 1),
                        (32 + 4 * (c // 2) + j, c % 2))]
    cw1 = given("cw1_dram", slices[[f for f, _ in order], [h for _, h in order]].reshape(BLOCKS, 2 * FB, H, G))
    def columns(v):
        return np.asarray(v).reshape(-1, P).T

    w1, b1 = given("w1_dram", r["W_top1"]), given("b1_dram", columns(r["b_top1"]))
    w2, b2 = given("w2_dram", r["W_top2"]), given("b2_dram", columns(r["b_top2"]))
    w3 = given("w3_dram", columns(r["W_top3"]))
    p = np.arange(P)
    delta = (p[:, None] % K == np.arange(K)[None]).astype(np.float32)
    quad = (p[:, None] // K == np.arange(NB)[None]).astype(np.float32)
    spread = quad[:, :, None] * np.tile(delta, (1, NB))[:, None, :]
    consts = given("consts_dram", np.concatenate([np.eye(P, dtype=np.float32), delta, quad,
                                                  spread.reshape(P, NB * P)], axis=1))
    x_scratch = nc.dram_tensor("x_scratch", (NB, B, FJ, 5 * H), F32, kind="Internal").ap()
    out = nc.dram_tensor("y_dram", (B, 1), F32, kind="ExternalOutput").ap()
    cin_tower(nc, ids, tables, dense, wa, wq1, wd, cw0, cw1, w1, b1, w2, b2, w3, consts, x_scratch, out)
    res = run(nc, [arrays], core_ids=[0])
    return res.results[0]["y_dram"]
```

```python
from contextlib import ExitStack

import concourse.bass as bass
from concourse import mybir

ALU = mybir.AluOpType
ACT = mybir.ActivationFunctionType
F32 = mybir.dt.float32
I32 = mybir.dt.int32
AX_X = mybir.AxisListType.X

P = 128
B, F, K, G = 512, 40, 32, 200
NB = P // K
FJ, FQ = P // K, F * K // P
C0 = F * F
NCH = -(-C0 // P)
TAIL = C0 - (NCH - 1) * P
GROUPS = [range(0, 4), range(4, 8), range(8, 11), range(11, NCH)]
PAIRS = B // (2 * NB)
H = G // 2
NDENSE, N1, N2 = 16, 512, 256
CHUNKS = B // P
BLOCKS, WIDE = NB * FJ, F * G // (NB * FJ)
SLICES = 4
DEEP = WIDE // SLICES
TURNS = BLOCKS
LAG = TURNS + 2
RING = 8
PLAIN = (1, 3, 5)
SHARED = 8 - len(PLAIN)
NORM = 3
LATE = (5, 6, 7)


def begun(i):
    return sum(j not in PLAIN for j in range(i + 1))


def scaled(i):
    return sum(j != NORM for j in range(i + 1))


def counts(n):
    return not isinstance(n, int) or n > 0


def run_turns(engine, turn, between):
    turn(-2, (2,))
    between(1)
    turn(-1, (1, 2))
    between(2)
    turn(0, (0, 1, 2))
    between(3)
    turn(1, (-1, 0, 1, 2))
    between(CHUNKS)
    for chunk, first, end in ((None, 2, LAG), (0, LAG, LAG + TURNS), (1, LAG + TURNS, LAG + 2 * TURNS),
                              (2, LAG + 2 * TURNS, PAIRS - 2)):
        with engine.Fori(first, end) as m:
            turn(m, (-1, 0, 1, 2), chunk)
    turn(PAIRS - 2, (-1, 0, 1), 2)
    turn(PAIRS - 1, (-1, 0), 2)
    turn(PAIRS, (-1,), 2)
    turn(PAIRS + 1, (), 2)


def cin_tower(nc, ids, tables, dense, wa, wq1, wd, cw0, cw1, w1, b1, w2, b2, w3, consts, x_scratch, out):
    with ExitStack() as ctx:
        def sb(name, shape, dt=F32):
            return ctx.enter_context(nc.sbuf_tensor(name, shape, dt))

        def bank(name):
            return ctx.enter_context(nc.psum_tensor(name, [P, 512], F32))

        def sem(name):
            return ctx.enter_context(nc.semaphore(name))

        cst = sb("cst", [P, P + K + NB + NB * P])
        ident = cst[:, 0:P]
        delta = cst[:, P:P + K]
        quad = cst[:, P + K:P + K + NB]
        spread = cst[:, P + K + NB:].rearrange("p (i m) -> p i m", i=NB)
        idx = sb("idx", [P, CHUNKS, F], I32)
        gath = sb("gath", [P, 2, F * K])
        e_field = sb("e_field", [P, B, FQ])
        e_row = sb("e_row", [P, 2, F])
        w_row = sb("w_row", [P, 4, F])
        w_field = sb("w_field", [P, 2, FQ])
        wq1_row = sb("wq1_row", [P, G])
        a0a1c0v0 = sb("a0a1c0v0", [P, 4, 2, F])
        ends = sb("ends", [P, 2, 2, 2])
        hold = sb("hold", [P, 2])
        mlo = sb("mlo", [P, 2, F])
        mhi = sb("mhi", [P, 2, F])
        m0 = sb("m0", [P, 2, F])
        x0 = sb("x0", [P, 2, C0])
        sum0 = sb("sum0", [P, F])
        rec0 = sb("rec0", [P, F])
        x0T = sb("x0T", [P, NCH, P])
        cw0_sb = sb("cw0_sb", [P, NCH, G])
        out0 = sb("out0", [P, G])
        low1 = sb("low1", [P, G])
        cm = sb("cm", [P, 2, 2, G])
        m_field = sb("m_field", [P, 2, G])
        a1 = sb("a1", [P, 8, FQ])
        v1 = sb("v1", [P, 8, FQ])
        ex = sb("ex", [P, 8, FQ * G])
        rec1 = sb("rec1", [P, G])
        rec_field = sb("rec_field", [P, 8, G])
        vsel = sb("vsel", [P, 8 * (FQ * 32 + 1)])
        xsum = sb("xsum", [P, WIDE])
        xq = sb("xq", [P, WIDE])
        xqT = sb("xqT", [DEEP, SLICES * P])
        cwq = sb("cwq", [DEEP, SLICES, G])
        z1 = sb("z1", [P, CHUNKS, G])
        z0T = sb("z0T", [H, 2, B])
        ring = ex[:].rearrange("p b x -> p (b x)")[:, 0:RING * (WIDE + SLICES * G)].rearrange(
            "p (r x) -> p r x", r=RING)
        xT = x0T[0:DEEP, 0:8, :].rearrange("p (a c) b -> p a (c b)", a=2)
        z1T = sb("z1T", [H, 2, B])
        w1_sb = sb("w1_sb", [H, 5, N1])
        w2_sb = sb("w2_sb", [P, N1 // P, N2])
        w3_sb = sb("w3_sb", [P, N2 // P])
        b1_sb = sb("b1_sb", [P, N1 // P])
        b2_sb = sb("b2_sb", [P, N2 // P])
        dense_sb = sb("dense_sb", [P, CHUNKS, NDENSE])
        denseT = sb("denseT", [NDENSE, B])
        h1T = gath[:].rearrange("p a b -> p (a b)")[:, 0:4 * 512].rearrange("p (c b) -> p c b", b=B)
        h2T = x0[:].rearrange("p a b -> p (a b)")[:, 0:2 * 512].rearrange("p (c b) -> p c b", b=B)
        y_sb = sb("y_sb", [1, B])

        pT = [bank("pT0"), bank("pT1")]
        pO = bank("pO")
        pC = [bank("pC0"), bank("pC1")]
        pS = bank("pS")
        pR = bank("pR")
        pX = bank("pX")

        pH = [pO, pT[0], pC[0], pC[1]]
        pL = [pT[1], pX]

        names = """loaded_idx loaded loaded_top gathered_even gathered_odd e_turned e_kept zeroed
            erow_made abc_made phi0_made phi0_shifted exp0_made x0_scaled x0_made
            x0_turned x0T_kept out0_made out0_kept z0_made z0_kept cm_made
            cm_spread m_kept a1_made products_made phi1_made exp1_made sums_made rec_made rec_spread rec_kept
            x1_by_pool x1_by_dve vsel_lo vsel_hi x_summed xsum_kept spilled
            hold_kept guard_step scale_step cm_step v1_made step_loaded step_turned step_kept
            step_made z1_added last_turned last_act last_dve last_made last_kept z1_turned z1_kept
            dense_turned dense_kept h1_made h1_kept h2_made h2_kept y_made y_kept y_stored"""
        s = {n: sem(n) for n in names.split()}

        gathered = [s["gathered_even"], s["gathered_odd"]]
        ring_loaded = [sem(f"ring_loaded_{r}") for r in range(RING)]

        vflat = vsel[:]
        vdiag = vflat.rearrange("p (b x) -> p b x", x=FQ * 32 + 1)[:, :, 0:FQ * 32].rearrange(
            "p b (f c) -> p b f c", c=32)[:, :, :, 0:32:8]
        ex4 = ex[:].rearrange("p b (f g) -> p b f g", g=G)
        n_loads = 6

        block = ctx.enter_context(nc.Block())

        @block.sync
        def _(sp):
            sp.dma_start(idx[:], ids.rearrange("(c p) f -> p c f", p=P)).then_inc(s["loaded_idx"], 16)
            for dst, src in ((cst[:], consts), (w_row[:], wa), (w_field[:], wd), (wq1_row[:], wq1),
                             (cw0_sb[:, 0:NCH - 1, :], cw0[0:(NCH - 1) * P, :].rearrange("(c p) j -> p c j", p=P)),
                             (cw0_sb[0:TAIL, NCH - 1, :], cw0[(NCH - 1) * P:, :])):
                sp.dma_start(dst, src).then_inc(s["loaded"], 16)
            for dst, src in ((w1_sb[:, 0:4, :], w1[0:4 * H, :].rearrange("(c p) j -> p c j", p=H)),
                             (w1_sb[0:NDENSE, 4, :], w1[4 * H:, :]),
                             (w2_sb[:], w2.rearrange("(c p) j -> p c j", p=P)),
                             (w3_sb[:], w3),
                             (b1_sb[:], b1),
                             (b2_sb[:], b2),
                             (dense_sb[:], dense.rearrange("(c p) j -> p c j", p=P))):
                sp.dma_start(dst, src).then_inc(s["loaded_top"], 16)

            def spill(k, i):
                sp.wait_ge(s["xsum_kept"], k * TURNS + i + 1)
                sp.dma_start(x_scratch[bass.ds(k * BLOCKS, BLOCKS), bass.ds(i * 8, 8), :],
                             xsum[:]).then_inc(s["spilled"], 16)

            def load_step(k, i):
                sp.wait_ge(s["spilled"], k * (16 * TURNS) + 16 * TURNS)
                sp.wait_ge(s["z1_added"], k * TURNS + i + 1)
                sp.dma_start(xq[:], x_scratch[bass.ds(k * BLOCKS + i, 1), :, :].rearrange("o b x -> (o b) x")
                             ).then_inc(s["step_loaded"], 16)
                sp.dma_start(cwq[:], cw1[bass.ds(i, 1), :, :, :].rearrange("o p u j -> (o p) u j")
                             ).then_inc(s["step_loaded"], 16)

            with sp.Fori(0, TURNS) as i:
                spill(0, i)
            with sp.Fori(1, CHUNKS) as k:
                with sp.Fori(0, TURNS) as i:
                    load_step(k - 1, i)
                    spill(k, i)

            def load_ring(i, what):
                r = i % RING
                if what == "cw":
                    if i >= RING:
                        sp.wait_ge(s["last_made"], i - RING + 1)
                    sp.dma_start(ring[0:DEEP, r, WIDE:].rearrange("p (u j) -> p u j", j=G),
                                 cw1[i]).then_inc(ring_loaded[r], 16)
                else:
                    sp.dma_start(ring[:, r, 0:WIDE],
                                 x_scratch[(CHUNKS - 1) * BLOCKS + i]).then_inc(ring_loaded[r], 16)

            early = NB * FQ * G // (WIDE + SLICES * G)
            sp.wait_ge(s["x_summed"], 8 * PAIRS - NB)
            for i in range(early):
                load_ring(i, "cw")
            sp.wait_ge(s["x_summed"], 8 * PAIRS)
            for i in range(early, RING):
                load_ring(i, "cw")
            sp.wait_ge(s["spilled"], 16 * PAIRS)
            for i in range(RING):
                load_ring(i, "x")
            for i in range(RING, BLOCKS):
                load_ring(i, "cw")
                load_ring(i, "x")
            sp.wait_ge(s["y_kept"], 1)
            sp.dma_start(out.rearrange("b o -> o b"), y_sb[:]).then_inc(s["y_stored"], 16)
            sp.wait_ge(s["y_stored"], 16)

        @block.gpsimd
        def _(pool):
            pool.wait_ge(s["loaded_idx"], 16)

            def gather(c, fields=range(F)):
                if c >= 2:
                    pool.wait_ge(s["e_turned"], 3 * (c - 1))
                for f in fields:
                    pool.indirect_dma_start(
                        out=gath[:, c % 2, f * K:(f + 1) * K], out_offset=None, in_=tables[f],
                        in_offset=bass.IndirectOffsetOnAxis(ap=idx[:, c, f:f + 1], axis=0),
                    ).then_inc(gathered[c % 2], 16)

            def weighted(p):
                pool.wait_ge(s["erow_made"], p + 1)
                if counts(p):
                    pool.wait_ge(s["x0_made"], p * 2)
                pool.tensor_tensor(a0a1c0v0[:], e_row[:].unsqueeze(1).to_broadcast([P, 4, 2, F]),
                                   w_row[:].unsqueeze(2).to_broadcast([P, 4, 2, F]),
                                   ALU.mult).then_inc(s["abc_made"], 1)
                pool.wait_ge(s["abc_made"], p + 1)

            def phi0(p, h):
                if counts(p):
                    pool.wait_ge(s["x0_turned"], (p * 2 + h - 1) * 4)
                pool.tensor_tensor(x0[:, h, :].rearrange("p (f g) -> p f g", g=F),
                                   a0a1c0v0[:, 0, h, :].unsqueeze(2).to_broadcast([P, F, F]),
                                   a0a1c0v0[:, 2, h, :].unsqueeze(1).to_broadcast([P, F, F]),
                                   ALU.mult).then_inc(s["phi0_made"], 1)

            def x0_values(p, h):
                pool.wait_ge(s["x0_scaled"], p * 2 + h + 1)
                v = x0[:, h, :].rearrange("p (f g) -> p f g", g=F)
                pool.tensor_tensor(v, v, a0a1c0v0[:, 3, h, :].unsqueeze(2).to_broadcast([P, F, F]),
                                   ALU.mult).then_inc(s["x0_made"], 1)

            def x1(p, i, live=()):
                if live == (-1,) and i in LATE:
                    return
                pool.wait_ge(s["rec_kept"], p * 4 + (i // 2 + 1))
                pool.tensor_tensor(ex4[:, i, :, :], ex4[:, i, :, :],
                                   rec_field[:, i, :].unsqueeze(1).to_broadcast([P, FQ, G]),
                                   ALU.mult).then_inc(s["x1_by_pool"], 1)

            def turn(m, live, chunk=None):
                if -1 in live:
                    x1(m - 1, 0)
                    x1(m - 1, 1)
                if 1 in live:
                    x0_values(m + 1, 0)
                if -1 in live:
                    x1(m - 1, 2)
                    x1(m - 1, 4)
                if 1 in live:
                    x0_values(m + 1, 1)
                if -1 in live:
                    x1(m - 1, 5, live)
                    x1(m - 1, 6, live)
                if 2 in live:
                    weighted(m + 2)
                if -1 in live:
                    x1(m - 1, 7, live)
                if 2 in live:
                    phi0(m + 2, 0)
                if live == (1, 2):
                    gather(2, first_part)
                if live == (0, 1, 2):
                    gather(3)
                if 2 in live:
                    phi0(m + 2, 1)

            first_part = range(10)

            def gather_rest(c):
                if c in (1, 2):
                    gather(c, range(first_part.stop, F))

            gather(0)
            gather(1, first_part)
            pool.wait_ge(s["loaded"], 16 * n_loads)
            run_turns(pool, turn, gather_rest)

        @block.vector
        def _(dve):
            def ends0(p):
                if counts(p):
                    dve.wait_ge(s["cm_made"], p * 2 - 1)
                    dve.tensor_copy(hold[:], ends[:, :, 1, 1]).then_inc(s["hold_kept"], 1)
                    dve.wait_ge(s["hold_kept"], p)
                dve.wait_ge(s["abc_made"], p + 1)
                a = a0a1c0v0[:, 0:2, :, :]
                dve.tensor_reduce(ends[:, 0, :, :], a, AX_X, ALU.max).then_inc(s["guard_step"], 1)
                dve.tensor_reduce(ends[:, 1, :, :], a, AX_X, ALU.min).then_inc(s["guard_step"], 1)

            def products0(p):
                dve.wait_ge(s["guard_step"], p * 5 + 2)
                c = a0a1c0v0[:, 2, :, :]
                dve.tensor_tensor(mhi[:], c, ends[:, 0, 0, :].unsqueeze(2).to_broadcast([P, 2, F]),
                                  ALU.mult).then_inc(s["guard_step"], 1)
                dve.tensor_tensor(mlo[:], c, ends[:, 1, 0, :].unsqueeze(2).to_broadcast([P, 2, F]),
                                  ALU.mult).then_inc(s["guard_step"], 1)

            def guard0(p):
                dve.wait_ge(s["guard_step"], p * 5 + 4)
                if counts(p):
                    dve.wait_ge(s["phi0_shifted"], p * 2)
                dve.tensor_tensor(m0[:], mhi[:], mlo[:], ALU.max).then_inc(s["guard_step"], 1)

            def shift0(p, h):
                dve.wait_ge(s["phi0_made"], p * 2 + h + 1)
                dve.wait_ge(s["guard_step"], p * 5 + 5)
                v = x0[:, h, :].rearrange("p (f g) -> p f g", g=F)
                dve.tensor_tensor(v, v, m0[:, h, :].unsqueeze(1).to_broadcast([P, F, F]),
                                  ALU.subtract).then_inc(s["phi0_shifted"], 1)

            def sum_0(p, h):
                t = p * 2 + h
                dve.wait_ge(s["exp0_made"], t + 1)
                if counts(t):
                    dve.wait_ge(s["scale_step"], t * 2)
                v = x0[:, h, :].rearrange("p (f g) -> p g f", g=F)
                dve.tensor_reduce(sum0[:], v, AX_X, ALU.add).then_inc(s["scale_step"], 1)

            def rec_0(p, h):
                t = p * 2 + h
                dve.wait_ge(s["scale_step"], t * 2 + 1)
                if counts(t):
                    dve.wait_ge(s["x0_scaled"], t)
                dve.reciprocal(rec0[:], sum0[:]).then_inc(s["scale_step"], 1)

            def scale0(p, h):
                dve.wait_ge(s["scale_step"], p * 4 + h * 2 + 2)
                v = x0[:, h, :].rearrange("p (f g) -> p f g", g=F)
                dve.tensor_tensor(v, v, rec0[:].unsqueeze(1).to_broadcast([P, F, F]),
                                  ALU.mult).then_inc(s["x0_scaled"], 1)

            def make_c(p, h):
                t = p * 2 + h
                dve.wait_ge(s["out0_kept"], t + 1)
                if counts(p):
                    dve.wait_ge(s["cm_spread"], p * 8 - 4 + 4 * h)
                dve.tensor_tensor(cm[:, h, 0, :], out0[:], wq1_row[:], ALU.mult).then_inc(s["cm_step"], 1)

            def ends1(h, last):
                return (hold[:, 0:1], hold[:, 1:2]) if h and not last else (ends[:, 0, 1, h:h + 1],
                                                                           ends[:, 1, 1, h:h + 1])

            def make_low(p, h, last=False):
                t = p * 2 + h
                dve.wait_ge(s["cm_step"], t * 2 + 1)
                if counts(t):
                    dve.wait_ge(s["cm_made"], t)
                dve.tensor_scalar(low1[:], cm[:, h, 0, :], ends1(h, last)[1], None,
                                  ALU.mult).then_inc(s["cm_step"], 1)

            def make_cm(p, h, last=False):
                dve.wait_ge(s["cm_step"], p * 4 + h * 2 + 2)
                dve.scalar_tensor_tensor(out=cm[:, h, 1, :], in0=cm[:, h, 0, :], scalar=ends1(h, last)[0],
                                         in1=low1[:], op0=ALU.mult, op1=ALU.max).then_inc(s["cm_made"], 1)

            def phi1(p, i):
                if i in PLAIN:
                    dve.wait_ge(s["m_kept"], p * 8 + i + 1)
                    dve.wait_ge(s["a1_made"], p * 2 + i // 4 + 1)
                    if counts(p):
                        dve.wait_ge(s["x_summed"], (p - 1) * 8 + i + 1)
                    for f in range(FQ):
                        ins = dve.scalar_tensor_tensor(out=ex4[:, i, f, :], in0=pC[i % 2][:, 0:G],
                                                       scalar=a1[:, i, f:f + 1], in1=m_field[:, i % 2, :],
                                                       op0=ALU.mult, op1=ALU.subtract)
                else:
                    dve.wait_ge(s["products_made"], p * SHARED + begun(i))
                    ins = dve.tensor_tensor(ex4[:, i, :, :], ex4[:, i, :, :],
                                            m_field[:, i % 2, :].unsqueeze(1).to_broadcast([P, FQ, G]),
                                            ALU.subtract)
                ins.then_inc(s["phi1_made"], 1)

            def rec_1(p, h):
                t = p * 2 + h
                dve.wait_ge(s["sums_made"], t + 1)
                if counts(t):
                    dve.wait_ge(s["rec_spread"], t * 2)
                dve.reciprocal(rec1[:], pS[:, 0:G]).then_inc(s["rec_made"], 1)

            def x1(p, i):
                dve.wait_ge(s["rec_kept"], p * 4 + (i // 2 + 1))
                dve.tensor_tensor(ex4[:, i, :, :], ex4[:, i, :, :],
                                  rec_field[:, i, :].unsqueeze(1).to_broadcast([P, FQ, G]),
                                  ALU.mult).then_inc(s["x1_by_dve"], 1)

            def a1_of(p, half):
                last = 4 * half + 3
                if counts(p):
                    dve.wait_ge(s["products_made"], (p - 1) * SHARED + begun(last))
                    dve.wait_ge(s["phi1_made"], (p - 1) * 8 + max(i for i in PLAIN if i <= last) + 1)
                dve.tensor_tensor(a1[:, 4 * half:4 * half + 4, :], e_field[:, bass.ds(p * 8 + 4 * half, 4), :],
                                  w_field[:, 0, :].unsqueeze(1).to_broadcast([P, 4, FQ]),
                                  ALU.mult).then_inc(s["a1_made"], 1)

            def v1_of(p):
                if counts(p):
                    dve.wait_ge(s["vsel_lo"], p)
                    dve.wait_ge(s["vsel_hi"], p)
                dve.tensor_tensor(v1[:], e_field[:, bass.ds(p * 8, 8), :],
                                  w_field[:, 1, :].unsqueeze(1).to_broadcast([P, 8, FQ]),
                                  ALU.mult).then_inc(s["v1_made"], 1)

            def keep_xT(q):
                dve.wait_ge(s["step_turned"], q + 1)
                dve.tensor_copy(xqT[:], pS[0:DEEP, :]).then_inc(s["step_kept"], 1)

            def add_z1(q, chunk):
                dve.wait_ge(s["step_made"], q + 1)
                dve.wait_ge(s["z1_added"], q + 1)
                dve.tensor_tensor(z1[:, chunk, :], z1[:, chunk, :], pS[:, 0:G], ALU.add).then_inc(s["z1_added"], 1)

            def vsel_write(p, half):
                dve.wait_ge(s["v1_made"], p + 1)
                if counts(p):
                    dve.wait_ge(s["x_summed"], (p - 1) * 8 + 4 * half + 4)
                b = slice(4 * half, 4 * half + 4)
                dve.tensor_tensor(vdiag[:, b, :, :], v1[:, b, :].unsqueeze(3).to_broadcast([P, 4, FQ, 4]),
                                  quad.unsqueeze(1).unsqueeze(1).to_broadcast([P, 4, FQ, 4]),
                                  ALU.mult).then_inc(s["vsel_hi" if half else "vsel_lo"], 1)

            def turn(m, live, chunk=None):
                if 1 in live:
                    rec_0(m + 1, 0)
                    scale0(m + 1, 0)
                if -1 in live:
                    x1(m - 1, 3)
                if 1 in live:
                    sum_0(m + 1, 1)
                if -1 in live:
                    rec_1(m - 1, 1)
                if 0 in live:
                    phi1(m, 0)
                    make_c(m, 1)
                if 1 in live:
                    rec_0(m + 1, 1)
                if -1 in live:
                    vsel_write(m - 1, 1)
                if live == (-1,):
                    for i in LATE:
                        x1(m - 1, i)
                if 1 in live:
                    scale0(m + 1, 1)
                if 0 in live:
                    make_low(m, 1, last=live == (-1, 0))
                    phi1(m, 1)
                    make_cm(m, 1, last=live == (-1, 0))
                    phi1(m, 2)
                    a1_of(m, 1)
                    phi1(m, 3)
                if chunk is not None:
                    keep_xT(m - LAG)
                if 0 in live:
                    phi1(m, 4)
                if 1 in live:
                    make_c(m + 1, 0)
                if 0 in live:
                    v1_of(m)
                if 1 in live:
                    make_low(m + 1, 0)
                if chunk is not None:
                    add_z1(m - LAG, chunk)
                if 1 in live:
                    make_cm(m + 1, 0)
                if 2 in live:
                    ends0(m + 2)
                if 0 in live:
                    phi1(m, 5)
                    vsel_write(m, 0)
                if 2 in live:
                    products0(m + 2)
                if 1 in live:
                    a1_of(m + 1, 0)
                if 2 in live:
                    guard0(m + 2)
                if 0 in live:
                    rec_1(m, 0)
                    phi1(m, 6)
                if 2 in live:
                    shift0(m + 2, 0)
                    shift0(m + 2, 1)
                if 0 in live:
                    phi1(m, 7)
                if 2 in live:
                    sum_0(m + 2, 0)

            dve.memset(vsel[:], 0.0).then_inc(s["zeroed"], 1)
            dve.memset(z1[:], 0.0).then_inc(s["z1_added"], 1)
            dve.wait_ge(s["zeroed"], 1)
            dve.wait_ge(s["loaded"], 16 * n_loads)
            dve.wait_ge(s["e_kept"], 3)

            def all_embeddings(c):
                if c == CHUNKS:
                    dve.wait_ge(s["e_kept"], 3 * CHUNKS)

            run_turns(dve, turn, all_embeddings)

            for i in range(1, BLOCKS, 2):
                dve.wait_ge(s["last_turned"], i + 1)
                dve.tensor_copy(xT[:, 1, :], pL[1][0:DEEP, :]).then_inc(s["last_dve"], 1)
            dve.wait_ge(s["last_made"], BLOCKS)
            dve.tensor_copy(z1[:, CHUNKS - 1, :], pR[:, 0:G]).then_inc(s["last_kept"], 1)

        @block.scalar
        def _(act):
            def keep_e(c):
                for g in range(3):
                    q0, q1 = 4 * g, min(4 * g + 4, FQ)
                    act.wait_ge(s["e_turned"], 3 * c + g + 1)
                    nc.scalar.copy(e_field[:, c * P:(c + 1) * P, q0:q1].rearrange("p b q -> p q b"),
                                   pX[:, 0:(q1 - q0) * P].rearrange("p (q b) -> p q b", b=P)
                                   ).then_inc(s["e_kept"], 1)

            def e_rows(p):
                if counts(p):
                    act.wait_ge(s["abc_made"], p)
                src = e_field[:, bass.ds(p * 8, 8), :].rearrange("p (s i) q -> p s i q", i=NB)
                dst = e_row[:].rearrange("p s (q j) -> p s q j", j=FJ)
                for i in range(NB):
                    for j in range(FJ):
                        ins = nc.scalar.copy(dst[K * i:K * i + K, :, :, j], src[K * j:K * j + K, :, i, :])
                ins.then_inc(s["erow_made"], 1)

            def exp0(p, h):
                act.wait_ge(s["phi0_shifted"], p * 2 + h + 1)
                nc.scalar.activation(x0[:, h, :], x0[:, h, :], ACT.Exp).then_inc(s["exp0_made"], 1)

            def keep_x0T(p, h, g):
                act.wait_ge(s["x0_turned"], (p * 2 + h) * 4 + g + 1)
                whole = [ch for ch in GROUPS[g] if ch < NCH - 1]
                ins = nc.scalar.copy(x0T[:, whole[0]:whole[-1] + 1, :],
                                     pT[g % 2][:, 0:len(whole) * P].rearrange("p (c b) -> p c b", b=P))
                if g == 3:
                    ins = nc.scalar.copy(x0T[0:TAIL, NCH - 1, :], pT[1][0:TAIL, P:2 * P])
                ins.then_inc(s["x0T_kept"], 1)

            def keep_out0(p, h):
                t = p * 2 + h
                act.wait_ge(s["out0_made"], t + 1)
                if counts(t):
                    act.wait_ge(s["cm_made"], t)
                nc.scalar.copy(out0[:], pO[:, 0:G]).then_inc(s["out0_kept"], 1)

            def keep_z0(p, h):
                t = p * 2 + h
                act.wait_ge(s["z0_made"], t + 1)
                nc.scalar.copy(z0T[:, :, bass.ds(t * 4, 4)],
                               pO[0:H, 256:264].rearrange("p (h b) -> p h b", b=4)).then_inc(s["z0_kept"], 1)

            def keep_m(p, i):
                act.wait_ge(s["cm_spread"], p * 8 + i + 1)
                n = p * 8 + i - 1
                if counts(n):
                    act.wait_ge(s["phi1_made"], n)
                nc.scalar.copy(m_field[:, i % 2, :], pC[i % 2][:, G:2 * G]).then_inc(s["m_kept"], 1)

            def products(p, i):
                act.wait_ge(s["a1_made"], p * 2 + i // 4 + 1)
                if counts(p):
                    act.wait_ge(s["x_summed"], (p - 1) * 8 + i + 1)
                for f in range(FQ):
                    ins = nc.scalar.activation(ex4[:, i, f, :], pC[i % 2][:, 0:G], ACT.Copy,
                                               scale=a1[:, i, f:f + 1])
                ins.then_inc(s["products_made"], 1)

            def exp1(p, i):
                act.wait_ge(s["phi1_made"], p * 8 + i + 1)
                nc.scalar.activation(ex[:, i, :], ex[:, i, :], ACT.Exp).then_inc(s["exp1_made"], 1)

            def keep_rec(p, i2):
                act.wait_ge(s["rec_spread"], p * 4 + i2 + 1)
                nc.scalar.copy(rec_field[:, 2 * i2:2 * i2 + 2, :],
                               pR[:, 0:2 * G].rearrange("p (b g) -> p b g", g=G)).then_inc(s["rec_kept"], 1)

            def keep_xsum(p):
                act.wait_ge(s["x_summed"], p * 8 + 8)
                if counts(p):
                    act.wait_ge(s["spilled"], p * 16)
                nc.scalar.copy(xsum[:], pX[:, 0:WIDE]).then_inc(s["xsum_kept"], 1)

            def turn(m, live, chunk=None):
                if -1 in live:
                    exp1(m - 1, 6)
                    exp1(m - 1, 7)
                if 0 in live:
                    keep_m(m, 0)
                    keep_m(m, 1)
                    keep_out0(m, 1)
                if -1 in live:
                    keep_rec(m - 1, 1)
                if 1 in live:
                    exp0(m + 1, 1)
                if 0 in live:
                    products(m, 0)
                if 1 in live:
                    keep_x0T(m + 1, 0, 0)
                if 2 in live:
                    e_rows(m + 2)
                if -1 in live:
                    keep_rec(m - 1, 2)
                if 1 in live:
                    keep_x0T(m + 1, 0, 1)
                if 0 in live:
                    keep_m(m, 2)
                    exp1(m, 0)
                if 1 in live:
                    keep_x0T(m + 1, 0, 2)
                    keep_x0T(m + 1, 0, 3)
                if 0 in live:
                    keep_z0(m, 1)
                    products(m, 2)
                if -1 in live:
                    keep_rec(m - 1, 3)
                if 0 in live:
                    exp1(m, 1)
                    keep_m(m, 3)
                if 1 in live:
                    keep_x0T(m + 1, 1, 0)
                if 0 in live:
                    keep_m(m, 4)
                    products(m, 4)
                if 1 in live:
                    keep_out0(m + 1, 0)
                if 0 in live:
                    exp1(m, 2)
                    exp1(m, 3)
                    keep_m(m, 5)
                    keep_m(m, 6)
                if 1 in live:
                    keep_x0T(m + 1, 1, 1)
                if 0 in live:
                    exp1(m, 4)
                    products(m, 6)
                    exp1(m, 5)
                if -1 in live:
                    keep_xsum(m - 1)
                if 1 in live:
                    keep_z0(m + 1, 0)
                    keep_x0T(m + 1, 1, 2)
                if 0 in live:
                    keep_m(m, 7)
                if 1 in live:
                    keep_x0T(m + 1, 1, 3)
                if 0 in live:
                    keep_rec(m, 0)
                    products(m, 7)
                if 2 in live:
                    exp0(m + 2, 0)

            keep_e(0)
            act.wait_ge(s["e_kept"], 3)
            act.wait_ge(s["dense_turned"], 1)
            nc.scalar.copy(denseT[:], pX[0:NDENSE, :]).then_inc(s["dense_kept"], 1)

            def keep_e_before(c):
                if c >= 2:
                    keep_e(c - 1)
                if c == CHUNKS:
                    act.wait_ge(s["e_kept"], 3 * CHUNKS)

            run_turns(act, turn, keep_e_before)

            def keep_z1T(h, b0, b1):
                act.wait_ge(s["z1_turned"], h + 1 if b0 == 0 else 3)
                nc.scalar.copy(z1T[:, h, b0:b1], pS[0:H, 0:b1] if b0 == 0 else pS[0:H, h * P:(h + 1) * P]
                               ).then_inc(s["z1_kept"], 1)

            keep_z1T(0, 0, B - P)
            keep_z1T(1, 0, B - P)
            for i in range(0, BLOCKS, 2):
                act.wait_ge(s["last_turned"], i + 1)
                nc.scalar.copy(xT[:, 0, :], pL[0][0:DEEP, :]).then_inc(s["last_act"], 1)
            keep_z1T(0, B - P, B)
            keep_z1T(1, B - P, B)
            for c in range(N1 // P):
                act.wait_ge(s["h1_made"], c + 1)
                nc.scalar.activation(h1T[:, c, :], pH[c][:, :], ACT.Relu,
                                     bias=b1_sb[:, c:c + 1]).then_inc(s["h1_kept"], 1)
            for c in range(N2 // P):
                act.wait_ge(s["h2_made"], c + 1)
                nc.scalar.activation(h2T[:, c, :], pL[c][:, :], ACT.Relu,
                                     bias=b2_sb[:, c:c + 1]).then_inc(s["h2_kept"], 1)
            act.wait_ge(s["y_made"], 1)
            nc.scalar.copy(y_sb[:], pS[0:1, :]).then_inc(s["y_kept"], 1)

        @block.tensor
        def _(pe):
            pe.wait_ge(s["loaded"], 16 * n_loads)
            pe.wait_ge(s["zeroed"], 1)

            def turn_e(c):
                pe.wait_ge(gathered[c % 2], 16 * F * (c // 2 + 1))
                for g in range(3):
                    if 3 * c + g:
                        pe.wait_ge(s["e_kept"], 3 * c + g)
                    for q in range(4 * g, min(4 * g + 4, FQ)):
                        ins = pe.transpose(pX[:, (q - 4 * g) * P:(q - 4 * g + 1) * P],
                                           gath[:, c % 2, q * P:(q + 1) * P], ident)
                    ins.then_inc(s["e_turned"], 1)

            def turn_x0(p, h, g):
                t = p * 2 + h
                pe.wait_ge(s["x0_made"], t + 1)
                n = t * 4 + g - 1
                if counts(n):
                    pe.wait_ge(s["x0T_kept"], n)
                for at, ch in enumerate(GROUPS[g]):
                    n = min(P, C0 - ch * P)
                    ins = pe.transpose(pT[g % 2][0:n, at * P:(at + 1) * P], x0[:, h, ch * P:ch * P + n], ident)
                ins.then_inc(s["x0_turned"], 1)

            def out0_of(p, h, g):
                t = p * 2 + h
                if g == 0 and counts(t):
                    pe.wait_ge(s["z0_kept"], t)
                pe.wait_ge(s["x0T_kept"], t * 4 + g + 1)
                for ch in GROUPS[g]:
                    n = min(P, C0 - ch * P)
                    ins = pe.matmul(pO[:, 0:G], x0T[0:n, ch, :], cw0_sb[0:n, ch, :],
                                    start=(ch == 0), stop=(ch == NCH - 1))
                if g == 3:
                    ins.then_inc(s["out0_made"], 1)

            def z0_of(p, h):
                pe.wait_ge(s["out0_kept"], p * 2 + h + 1)
                for j in range(2):
                    ins = pe.matmul(pO[0:H, 256 + 4 * j:260 + 4 * j], out0[:, j * H:(j + 1) * H], quad,
                                    start=True, stop=True)
                ins.then_inc(s["z0_made"], 1)

            def spread_cm(p, i):
                pe.wait_ge(s["cm_made"], p * 2 + (i // 4 + 1))
                before, j = (p, i - 2) if i >= 2 else (p - 1, i + 6)
                if not isinstance(before, int) or before >= 0:
                    if j in PLAIN:
                        pe.wait_ge(s["phi1_made"], before * 8 + j + 1)
                    else:
                        pe.wait_ge(s["products_made"], before * SHARED + begun(j))
                pe.matmul(pC[i % 2][:, 0:2 * G], spread[:, i % 4, :],
                          cm[:, i // 4, :, :].rearrange("p a g -> p (a g)"),
                          start=True, stop=True).then_inc(s["cm_spread"], 1)

            def sums_of(p, half, step=False):
                t = p * 2 + half
                if step:
                    pe.wait_ge(s["z1_added"], p - LAG + 2)
                pe.wait_ge(s["exp1_made"], p * 8 + 4 * half + 4)
                if counts(t):
                    pe.wait_ge(s["rec_made"], t)
                for f in range(FQ):
                    for i in range(NB):
                        ins = pe.matmul(pS[K * i:K * i + K, 0:G], delta, ex4[:, 4 * half + i, f, :],
                                        start=(f == 0), stop=(f == FQ - 1), skip_group_check=True)
                ins.then_inc(s["sums_made"], 1)

            def spread_rec(p, i2):
                pe.wait_ge(s["rec_made"], p * 2 + (i2 // 2 + 1))
                n = p * 4 + i2
                if counts(n):
                    pe.wait_ge(s["rec_kept"], n)
                for b in range(2):
                    ins = pe.matmul(pR[:, b * G:(b + 1) * G], spread[:, (2 * i2 + b) % 4, :], rec1[:],
                                    start=True, stop=True)
                ins.then_inc(s["rec_spread"], 1)

            def xsum_of(p, i):
                if i == NORM:
                    pe.wait_ge(s["x1_by_dve"], p + 1)
                elif isinstance(p, int) and p == PAIRS - 1 and i in LATE:
                    pe.wait_ge(s["x1_by_dve"], PAIRS + LATE.index(i) + 1)
                else:
                    pe.wait_ge(s["x1_by_pool"], p * 7 + scaled(i))
                pe.wait_ge(s["vsel_lo" if i < 4 else "vsel_hi"], p + 1)
                if i == 0 and counts(p):
                    pe.wait_ge(s["xsum_kept"], p)
                w = vflat[:, i * FQ * 32:(i + 1) * FQ * 32].rearrange("p (f c) -> p f c", c=32)
                for slot in range(3):
                    for c in range(4):
                        f = 4 * slot + c if slot < 2 else 8 + c // 2
                        g0, n = (0, G) if slot < 2 else (H * (c % 2), H)
                        ins = pe.matmul(pX[32 * c:32 * c + 32, slot * G:slot * G + n], w[:, f, :],
                                        ex4[:, i, f, g0:g0 + n], start=(i == 0 and slot == 0),
                                        stop=(i == 7 and slot == 2), skip_group_check=True)
                ins.then_inc(s["x_summed"], 1)

            def turn_sums(q):
                pe.wait_ge(s["step_loaded"], q * 32 + 32)
                sums = q * 2 + 2 * LAG
                if isinstance(sums, int):
                    sums = min(sums, 2 * PAIRS)
                pe.wait_ge(s["rec_made"], sums)
                for u in range(SLICES):
                    ins = pe.transpose(pS[0:DEEP, u * P:(u + 1) * P], xq[:, u * DEEP:(u + 1) * DEEP], ident)
                ins.then_inc(s["step_turned"], 1)

            def contract(q):
                pe.wait_ge(s["step_kept"], q + 1)
                for u in range(SLICES):
                    ins = pe.matmul(pS[:, 0:G], xqT[:, u * P:(u + 1) * P], cwq[:, u, :],
                                    start=(u == 0), stop=(u == SLICES - 1))
                ins.then_inc(s["step_made"], 1)

            def top1(r, z, b0=0, first=False, last=False):
                for c in range(N1 // P):
                    n = z.shape[0]
                    ins = pe.matmul(pH[c][:, b0:b0 + z.shape[1]], w1_sb[0:n, r, c * P:(c + 1) * P], z,
                                    start=first, stop=last, skip_group_check=True)
                    if last:
                        ins.then_inc(s["h1_made"], 1)

            def top1_early():
                pe.wait_ge(s["z0_kept"], 2 * PAIRS)
                pe.wait_ge(s["x0T_kept"], 8 * PAIRS)
                pe.wait_ge(s["products_made"], SHARED * PAIRS)
                pe.wait_ge(s["phi1_made"], 8 * PAIRS)
                top1(0, z0T[:, 0, :], first=True)
                top1(1, z0T[:, 1, :])
                top1(4, denseT[:])

            def turn(m, live, chunk=None):
                if live == ():
                    top1_early()
                if 0 in live:
                    out0_of(m, 1, 0)
                    out0_of(m, 1, 1)
                    out0_of(m, 1, 2)
                    out0_of(m, 1, 3)
                    spread_cm(m, 0)
                if -1 in live:
                    spread_rec(m - 1, 1)
                    xsum_of(m - 1, 0)
                if 0 in live:
                    spread_cm(m, 1)
                if -1 in live:
                    sums_of(m - 1, 1)
                if 1 in live:
                    turn_x0(m + 1, 0, 0)
                if -1 in live:
                    xsum_of(m - 1, 1)
                if 1 in live:
                    turn_x0(m + 1, 0, 1)
                if -1 in live:
                    spread_rec(m - 1, 2)
                if 0 in live:
                    spread_cm(m, 2)
                    z0_of(m, 1)
                if 1 in live:
                    turn_x0(m + 1, 0, 2)
                    turn_x0(m + 1, 0, 3)
                if -1 in live:
                    xsum_of(m - 1, 2)
                if chunk is not None:
                    turn_sums(m - LAG)
                if -1 in live:
                    spread_rec(m - 1, 3)
                    xsum_of(m - 1, 3)
                if 1 in live:
                    out0_of(m + 1, 0, 0)
                if -1 in live:
                    xsum_of(m - 1, 4)
                if 0 in live:
                    spread_cm(m, 3)
                    spread_cm(m, 4)
                if 1 in live:
                    turn_x0(m + 1, 1, 0)
                    out0_of(m + 1, 0, 1)
                    turn_x0(m + 1, 1, 1)
                    out0_of(m + 1, 0, 2)
                    out0_of(m + 1, 0, 3)
                if -1 in live:
                    xsum_of(m - 1, 5)
                if 0 in live:
                    spread_cm(m, 5)
                if chunk is not None:
                    contract(m - LAG)
                if 0 in live:
                    spread_cm(m, 6)
                if -1 in live:
                    xsum_of(m - 1, 6)
                if 0 in live:
                    sums_of(m, 0, chunk is not None)
                if 1 in live:
                    z0_of(m + 1, 0)
                    turn_x0(m + 1, 1, 2)
                if -1 in live:
                    xsum_of(m - 1, 7)
                if 1 in live:
                    turn_x0(m + 1, 1, 3)
                if 0 in live:
                    spread_cm(m, 7)
                    spread_rec(m, 0)

            turn_e(0)
            pe.wait_ge(s["e_kept"], 3)
            pe.wait_ge(s["loaded_top"], 16 * 7)
            for c in range(CHUNKS):
                ins = pe.transpose(pX[0:NDENSE, c * P:(c + 1) * P], dense_sb[:, c, :], ident)
            ins.then_inc(s["dense_turned"], 1)
            pe.wait_ge(s["dense_kept"], 1)

            def turn_e_before(c):
                if c == CHUNKS:
                    pe.wait_ge(s["xsum_kept"], 1)
                if c >= 2:
                    turn_e(c - 1)
                    pe.wait_ge(s["e_kept"], 3 * c)

            run_turns(pe, turn, turn_e_before)

            pe.wait_ge(s["rec_kept"], 4 * PAIRS)
            pe.wait_ge(s["xsum_kept"], PAIRS)
            pe.wait_ge(s["z1_added"], PAIRS - TURNS + 1)
            for h in range(2):
                if h:
                    pe.wait_ge(s["z1_kept"], 1)
                for c in range(CHUNKS - 1):
                    ins = pe.transpose(pS[0:H, c * P:(c + 1) * P], z1[:, c, h * H:(h + 1) * H], ident)
                ins.then_inc(s["z1_turned"], 1)
            for h in range(2):
                pe.wait_ge(s["z1_kept"], h + 1)
                top1(2 + h, z1T[:, h, 0:B - P])

            def turn_last(i):
                pe.wait_ge(ring_loaded[i % RING], 32 * (i // RING + 1))
                if i >= 2:
                    pe.wait_ge(s["last_dve" if i % 2 else "last_act"], i // 2)
                for u in range(SLICES):
                    ins = pe.transpose(pL[i % 2][0:DEEP, u * P:(u + 1) * P],
                                       ring[:, i % RING, u * DEEP:(u + 1) * DEEP], ident)
                ins.then_inc(s["last_turned"], 1)

            def contract_last(i):
                pe.wait_ge(s["last_dve" if i % 2 else "last_act"], i // 2 + 1)
                for u in range(SLICES):
                    ins = pe.matmul(pR[:, 0:G], xT[:, i % 2, u * P:(u + 1) * P],
                                    ring[0:DEEP, i % RING, WIDE + u * G:WIDE + (u + 1) * G],
                                    start=(i == 0 and u == 0), stop=(i == BLOCKS - 1 and u == SLICES - 1))
                ins.then_inc(s["last_made"], 1)

            turn_last(0)
            for i in range(BLOCKS):
                if i + 1 < BLOCKS:
                    turn_last(i + 1)
                contract_last(i)
            pe.wait_ge(s["last_kept"], 1)
            for h in range(2):
                ins = pe.transpose(pS[0:H, h * P:(h + 1) * P], z1[:, CHUNKS - 1, h * H:(h + 1) * H], ident)
            ins.then_inc(s["z1_turned"], 1)
            for h in range(2):
                pe.wait_ge(s["z1_kept"], 3 + h)
                top1(2 + h, z1T[:, h, B - P:B], b0=B - P, last=(h == 1))
            pe.wait_ge(s["h1_kept"], 4)
            for c in range(N2 // P):
                for r in range(N1 // P):
                    ins = pe.matmul(pL[c][:, :], w2_sb[:, r, c * P:(c + 1) * P], h1T[:, r, :],
                                    start=(r == 0), stop=(r == N1 // P - 1))
                ins.then_inc(s["h2_made"], 1)
            pe.wait_ge(s["h2_kept"], 2)
            for r in range(N2 // P):
                ins = pe.matmul(pS[0:1, :], w3_sb[:, r:r + 1], h2T[:, r, :], start=(r == 0), stop=(r == 1))
            ins.then_inc(s["y_made"], 1)


def kernel(**inputs):
    import numpy as np
    import concourse.bacc as bacc
    from concourse.bass_utils import run_bass_kernel_spmd as run

    nc = bacc.Bacc("TRN2", target_bir_lowering=False, num_devices=1)
    arrays = {}

    def given(name, a):
        a = np.ascontiguousarray(a)
        arrays[name] = a
        return nc.dram_tensor(name, a.shape, mybir.dt.from_np(a.dtype), kind="ExternalInput").ap()

    def rows(w):
        return np.tile(np.asarray(w)[0].T, (NB, 1))

    def fields(w):
        return np.asarray(w)[0].reshape(FQ, FJ, K).transpose(1, 2, 0).reshape(P, FQ)

    r = inputs
    ids = given("ids_dram", r["ids"])
    tables = [given(f"tbl_{f}_dram", r[f"tbl_{f}"]) for f in range(F)]
    dense = given("dense_dram", r["dense_ctx"])
    wa = given("wa_dram", np.stack([rows(r["L0_rec_wk0"]), rows(r["L0_rec_wk1"]), rows(r["L0_rec_wq0"]),
                                    rows(r["L0_rec_wv0"])], axis=1))
    wq1 = given("wq1_dram", rows(r["L0_rec_wq1"]))
    wd = given("wd_dram", np.stack([fields(r["L0_rec_wk1"]), fields(r["L0_rec_wv1"])], axis=1))
    cw0 = given("cw0_dram", np.asarray(r["L0_rec_cw0"])[0])
    w = np.asarray(r["L0_rec_cw1"])[0].reshape(F, 2, H, G)
    blocks = [np.concatenate([w[4 * c + j].reshape(2 * H, G), w[16 + 4 * c + j].reshape(2 * H, G),
                              w[32 + 4 * (c // 2) + j, c % 2]]) for c in range(NB) for j in range(FJ)]
    cw1 = given("cw1_dram", np.stack(blocks).reshape(BLOCKS, SLICES, DEEP, G).transpose(0, 2, 1, 3))

    def columns(v):
        return np.asarray(v).reshape(-1, P).T

    w1, b1 = given("w1_dram", r["W_top1"]), given("b1_dram", columns(r["b_top1"]))
    w2, b2 = given("w2_dram", r["W_top2"]), given("b2_dram", columns(r["b_top2"]))
    w3 = given("w3_dram", columns(r["W_top3"]))
    p = np.arange(P)
    delta = (p[:, None] % K == np.arange(K)[None]).astype(np.float32)
    quad = (p[:, None] // K == np.arange(NB)[None]).astype(np.float32)
    spread = quad[:, :, None] * np.tile(delta, (1, NB))[:, None, :]
    consts = given("consts_dram", np.concatenate([np.eye(P, dtype=np.float32), delta, quad,
                                                  spread.reshape(P, NB * P)], axis=1))
    x_scratch = nc.dram_tensor("x_scratch", (CHUNKS * BLOCKS, P, WIDE), F32, kind="Internal").ap()
    out = nc.dram_tensor("y_dram", (B, 1), F32, kind="ExternalOutput").ap()
    cin_tower(nc, ids, tables, dense, wa, wq1, wd, cw0, cw1, w1, b1, w2, b2, w3, consts, x_scratch, out)
    res = run(nc, [arrays], core_ids=[0])
    return res.results[0]["y_dram"]
```
